# Optimizing a Trainium2 kernel written in Bass

```python
import numpy as np
import jax
import jax.numpy as jnp

def _softmax(x, axis=-1):
    return jax.nn.softmax(x, axis=axis)

def _gelu(x):
    return jax.nn.gelu(x, approximate=True)

def _silu(x):
    return jax.nn.silu(x)

def _sigmoid(x):
    return jax.nn.sigmoid(x)

def _layernorm(x, axis=-1, eps=1e-05):
    m = jnp.mean(x, axis=axis, keepdims=True)
    v = jnp.var(x, axis=axis, keepdims=True)
    return (x - m) / jnp.sqrt(v + eps)

def _scatter_add(tgt, idx, src, axis=0):
    return tgt.at[idx].add(src)

def _segment_sum(src, seg, n):
    return jax.ops.segment_sum(src, seg, n)
kernel_name = 'mk_cond_resid_d4_seqx_r4_c98ce7'

def setup_inputs(seed: int=0):
    np.random.seed(seed)
    _w = jnp.asarray

    def _rec_inputs():
        import jax
        import jax.numpy as jnp
        _rk = jax.random.key(seed)
        x = -7.109e-05 + 0.9999 * jax.random.normal(jax.random.fold_in(_rk, 1), (32, 64, 1024), jnp.float32)
        _lenS = 64 - jax.random.randint(jax.random.fold_in(_rk, 7), (32,), 0, max(1, 64 // 4) + 1, jnp.int32)
        _lenS2 = 64 - jax.random.randint(jax.random.fold_in(_rk, 8), (32,), 0, max(1, 64 // 4) + 1, jnp.int32)
        itok_B_0_15 = jax.random.randint(jax.random.fold_in(_rk, 11), (32,), 0, 16, jnp.int32)
        itok_B_0_2 = jax.random.randint(jax.random.fold_in(_rk, 12), (32,), 0, 3, jnp.int32)
        itok_B_0_7 = jax.random.randint(jax.random.fold_in(_rk, 13), (32,), 0, 8, jnp.int32)
        return (x, itok_B_0_15, itok_B_0_2, itok_B_0_7)
    x, itok_B_0_15, itok_B_0_2, itok_B_0_7 = _rec_inputs()

    def _L0_cond_setup():
        import jax, jax.numpy as jnp
        import numpy as np
        B, C, T = (64, 64, 1024)
        S, D = (16, 64)
        key = jax.random.key(seed)
        k1, k2, k3 = jax.random.split(key, 3)
        x = jax.random.normal(k1, (B, C, T), dtype=jnp.float32)
        condition = jax.random.randint(k2, (B,), 0, S, dtype=jnp.int64)
        bound = float(np.sqrt(6.0 / C))
        weights = jax.random.uniform(k3, (S, C, D), dtype=jnp.float32, minval=-bound, maxval=bound)
        return {'x': x, 'condition': condition, 'weights': weights}
    _L0_cond_all = _L0_cond_setup()
    _L0_cond_in = {k: v for k, v in _L0_cond_all.items() if k in ('weights',)}
    del _L0_cond_all

    def _L1_cond_setup():
        import jax, jax.numpy as jnp
        import numpy as np
        SCALING = 16.0 / 16
        key = jax.random.key(seed)
        k1, k2, k3, k4, k5 = jax.random.split(key, 5)
        B, S, D_IN, D_OUT, R, N_ADPT = (8, 512, 1024, 1024, 16, 16)
        x = jax.random.normal(k1, (B, S, D_IN), dtype=jnp.float32)
        adapter_indices = jax.random.randint(k2, (B,), 0, N_ADPT, dtype=jnp.int32)
        W = jax.random.normal(k3, (D_IN, D_OUT), dtype=jnp.float32) * 0.02
        lora_A = jax.random.normal(k4, (N_ADPT, D_IN, R), dtype=jnp.float32) * 0.02
        lora_B = jax.random.normal(k5, (N_ADPT, R, D_OUT), dtype=jnp.float32) * 0.02
        return {'x': x, 'adapter_indices': adapter_indices, 'W': W, 'lora_A': lora_A, 'lora_B': lora_B}
    _L1_cond_all = _L1_cond_setup()
    _L1_cond_in = {k: v for k, v in _L1_cond_all.items() if k in ('W', 'lora_A', 'lora_B')}
    del _L1_cond_all

    def _L2_cond_setup():
        import jax, jax.numpy as jnp
        import numpy as np
        B, S, D_IN, D_OUT = (4, 512, 1024, 1024)
        R, NUM_LABELERS = (32, 5)
        LORA_SCALING = 16 / 32
        key = jax.random.key(seed)
        k1, k2, k3, k4, k5 = jax.random.split(key, 5)
        x = jax.random.normal(k1, (B, S, D_IN), dtype=jnp.float32)
        labeler_index = jax.random.randint(k2, (B,), 0, NUM_LABELERS, dtype=jnp.int64)
        W = jax.random.normal(k3, (D_OUT, D_IN), dtype=jnp.float32) * 0.02
        lora_A = jax.random.normal(k4, (NUM_LABELERS, D_IN, R), dtype=jnp.float32) * 0.02
        lora_B_w = jax.random.normal(k5, (D_OUT, R), dtype=jnp.float32) * 0.02
        return {'x': x, 'labeler_index': labeler_index, 'W': W, 'lora_A': lora_A, 'lora_B_w': lora_B_w}
    _L2_cond_all = _L2_cond_setup()
    _L2_cond_in = {k: v for k, v in _L2_cond_all.items() if k in ('W', 'lora_A', 'lora_B_w')}
    del _L2_cond_all

    def _L3_cond_setup():
        import jax, jax.numpy as jnp
        import numpy as np
        TOP_K = 2
        LANG_BIAS = 5.0
        SCALING = 32.0 / 16.0
        LANGUAGE_PAD_ID = -1
        key = jax.random.key(seed)
        ks = jax.random.split(key, 6)
        B, T, D, O, E, R = (4, 512, 1024, 1024, 8, 16)
        x = jax.random.normal(ks[0], (B, T, D), dtype=jnp.float32)
        language_ids = jax.random.randint(ks[1], (B,), 0, E).astype(jnp.int64)
        W = jax.random.normal(ks[2], (O, D), dtype=jnp.float32) * (1.0 / np.sqrt(D))
        Wr = jax.random.normal(ks[3], (E, D), dtype=jnp.float32) * (1.0 / np.sqrt(D))
        A = jax.random.normal(ks[4], (E, R, D), dtype=jnp.float32) * (1.0 / np.sqrt(D))
        Bm = jax.random.normal(ks[5], (O, R), dtype=jnp.float32) * 0.0
        Bm = jnp.broadcast_to(Bm, (E, O, R)) + jax.random.normal(ks[5], (E, O, R), dtype=jnp.float32) * 0.02
        return {'x': x, 'language_ids': language_ids, 'W': W, 'Wr': Wr, 'A': A, 'B': Bm}
    _L3_cond_all = _L3_cond_setup()
    _L3_cond_in = {k: v for k, v in _L3_cond_all.items() if k in ('W', 'Wr', 'A', 'B')}
    del _L3_cond_all
    return {'x': x, 'itok_B_0_15': itok_B_0_15, 'itok_B_0_2': itok_B_0_2, 'itok_B_0_7': itok_B_0_7, 'L0_cond_weights': _L0_cond_in['weights'], 'L1_cond_W': _L1_cond_in['W'], 'L1_cond_lora_A': _L1_cond_in['lora_A'], 'L1_cond_lora_B': _L1_cond_in['lora_B'], 'L2_cond_W': _L2_cond_in['W'], 'L2_cond_lora_A': _L2_cond_in['lora_A'], 'L2_cond_lora_B_w': _L2_cond_in['lora_B_w'], 'L3_cond_W': _L3_cond_in['W'], 'L3_cond_Wr': _L3_cond_in['Wr'], 'L3_cond_A': _L3_cond_in['A'], 'L3_cond_B': _L3_cond_in['B']}

def reference(x, itok_B_0_15, itok_B_0_2, itok_B_0_7, L0_cond_weights, L1_cond_W, L1_cond_lora_A, L1_cond_lora_B, L2_cond_W, L2_cond_lora_A, L2_cond_lora_B_w, L3_cond_W, L3_cond_Wr, L3_cond_A, L3_cond_B):
    import jax
    import jax.numpy as jnp

    def _L0_cond_ref(x, condition, weights):
        import jax, jax.numpy as jnp
        import numpy as np
        B, C, T = (64, 64, 1024)
        S, D = (16, 64)
        W = weights[condition]
        return jnp.einsum('bct,bcd->bdt', x, W)

    def _L1_cond_ref(x, adapter_indices, W, lora_A, lora_B):
        import jax, jax.numpy as jnp
        import numpy as np
        SCALING = 16.0 / 16
        base_out = jnp.einsum('bsi,io->bso', x, W)
        A = lora_A[adapter_indices]
        Bm = lora_B[adapter_indices]
        xr = jnp.einsum('bsi,bir->bsr', x, A)
        lora_out = jnp.einsum('bsr,bro->bso', xr, Bm)
        return base_out + lora_out * SCALING

    def _L2_cond_ref(x, labeler_index, W, lora_A, lora_B_w):
        import jax, jax.numpy as jnp
        import numpy as np
        B, S, D_IN, D_OUT = (4, 512, 1024, 1024)
        R, NUM_LABELERS = (32, 5)
        LORA_SCALING = 16 / 32
        base = jnp.einsum('bsi,oi->bso', x, W)
        labelers_A = lora_A[labeler_index]
        low = jnp.einsum('bsi,bir->bsr', x, labelers_A)
        delta = jnp.einsum('bsr,or->bso', low, lora_B_w) * LORA_SCALING
        return base + delta

    def _L3_cond_ref(x, language_ids, W, Wr, A, B):
        import jax, jax.numpy as jnp
        import numpy as np
        TOP_K = 2
        LANG_BIAS = 5.0
        SCALING = 32.0 / 16.0
        LANGUAGE_PAD_ID = -1
        base = jnp.einsum('btd,od->bto', x, W)
        E = Wr.shape[0]
        logits = jnp.einsum('btd,ed->bte', x.astype(jnp.float32), Wr.astype(jnp.float32))
        expert_targets = language_ids
        valid = expert_targets >= 0
        tgt = jnp.where(valid, expert_targets, 0)
        bias = jax.nn.one_hot(tgt, E, dtype=logits.dtype) * LANG_BIAS
        bias = jnp.where(valid[:, None], bias, 0.0)
        logits = logits + bias[:, None, :]
        topw, topi = jax.lax.top_k(logits, TOP_K)
        weights = jax.nn.softmax(topw, axis=-1)
        gates = jnp.sum(jax.nn.one_hot(topi, E, dtype=weights.dtype) * weights[..., None], axis=-2)
        gates = gates.astype(x.dtype)
        h = jnp.einsum('btd,erd->bter', x, A)
        lora_out = jnp.einsum('bter,bte,eor->bto', h, gates, B)
        return base + SCALING * lora_out
    x = x + _L0_cond_ref(x, itok_B_0_15, L0_cond_weights)
    x = x + _L1_cond_ref(x, itok_B_0_15, L1_cond_W, L1_cond_lora_A, L1_cond_lora_B)
    x = x + _L2_cond_ref(x, itok_B_0_2, L2_cond_W, L2_cond_lora_A, L2_cond_lora_B_w)
    x = x + _L3_cond_ref(x, itok_B_0_7, L3_cond_W, L3_cond_Wr, L3_cond_A, L3_cond_B)
    return x

_drawn_inputs = setup_inputs


def setup_inputs(seed=0):
    import zlib

    import numpy as np

    out = dict(_drawn_inputs(seed))
    spreads = {}
    factors = {'L2_cond_lora_A': 2.927, 'L2_cond_lora_B_w': 2.919}
    for name, (base, spread) in spreads.items():
        noise = np.random.default_rng([zlib.crc32(name.encode()), seed]).standard_normal(out[name].shape)
        drawn = base * np.exp(spread * noise) if base else spread * noise
        out[name] = jnp.asarray(drawn.astype(out[name].dtype))
    for name, factor in factors.items():
        out[name] = (out[name] * factor).astype(out[name].dtype)
    return out
```

```python
from contextlib import ExitStack

import concourse.bass as bass
from concourse import mybir

F32 = mybir.dt.float32
F32R = mybir.dt.float32r
I32 = mybir.dt.int32
U32 = mybir.dt.uint32
ALU = mybir.AluOpType
ACT = mybir.ActivationFunctionType

P = 128
BANK = 512
LANG_BIAS = 5.0
SCALE2 = 16 / 32
SCALE3 = 32.0 / 16.0


def cond_resid_kernel(nc, x, idx_adapter, idx_labeler, idx_language, w0, w1, a1, b1, w2, a2, b2, w3, wr, a3, b3, out):
    B, T, D = x.shape
    NA, _, R1 = a1.shape
    NL, _, R2 = a2.shape
    E, R3, _ = a3.shape
    K = D // P
    PER = P // T
    NB = B // PER
    assert PER == 2 and K == 8 and D == 2 * BANK and E * R3 == P and NB % 2 == 0
    ER = E * R3
    C3 = ER + E
    A2C = NL * R2
    EC = C3 + A2C
    XC = D + EC
    SC = C3 + PER * (R2 + R1)
    SEG1 = 3 * R1
    SEG2 = 3 * R2
    LORA = NA * R1 // P
    ROWS = LORA + K
    F3C = 3 * P
    FCOLS = [(0, F3C), (F3C, 2 * F3C), (2 * F3C, D)]
    WIDTH_A = [F3C, F3C, D - 2 * F3C + C3]
    LABELERS = [range(3, NL), range(0), range(0, 3)]
    WIDTH = [w + R2 * len(n) for w, n in zip(WIDTH_A, LABELERS)]
    ORDER = [2, 0, 1]
    ACC_A = 3 * (K + 1)
    ACC_B = 3 * ROWS

    def f32(ap):
        return ap.bitcast(F32)

    def above(engine, semaphore, value):
        if not isinstance(value, int) or value > 0:
            engine.wait_ge(semaphore, value)

    def held(engine, value):
        if isinstance(value, int):
            return value
        register = engine.alloc_register()
        engine.reg_mov(register, value)
        return engine.snap(register)

    BASE = 16512
    X0, Y0, Z0 = BASE, BASE + 65536, BASE + 150016
    R0 = Z0 + 35328
    V0 = R0 + 3 * 4096
    Q0 = V0 + 8192

    def at(name, shape, dtype, offset):
        return nc.alloc_sbuf_tensor_at(name, shape, dtype, offset=offset)

    def pair(name, shape, offset):
        size = 4
        for n in shape[1:]:
            size *= n
        return at(name + "_hi", shape, F32R, offset), at(name + "_lo", shape, F32R, offset + size)

    EY = [Y0, Y0 + 8 * K * WIDTH[0], Y0 + 8 * K * (WIDTH[0] + WIDTH[1])]
    W2S = pair("w2s", [P, K, D], X0)
    M = pair("m", [P, K, D], X0)
    EX = [pair(f"e{c}", [P, K, WIDTH[c]], EY[c]) for c in range(3)]
    G = [pair(f"g{c}", [P, K, WIDTH_A[c]], at_) for c, at_ in enumerate((EY[1], Z0, EY[0]))]
    w2raw = [at(f"w2raw{k}", [P, D], F32, Z0 + 4096 * k) for k in range(K)]
    early = [at(f"early{n}", [P, D], F32, EY[2] + 4096 * n) for n in range(2)]
    TB = pair("tb", [P, K, EC], Z0)
    W1T = [pair("w1t0", [P, K, P], Z0 + 27136), pair("w1t1", [P, K, P], Z0 + 18944)]
    ost = [at(f"ost{s}", [P, D], F32, Z0 + 18944 + 4096 * s) for s in range(2)]
    raw = [at(f"raw{n}", [P, D], F32, R0 + 4096 * n) for n in range(3)]
    b1stage = [pair(f"b1stage{n}", [P, BANK], X0 + 4 * D * (K - 3 + n + (K - 3) * (n // 3))) for n in range(3 * LORA)]
    bdraw = [at(f"bdraw{s}", [P, P], F32, R0 + 8192 + 512 * s) for s in range(2)]
    BD = pair("bd", [P, P], R0 + 9216)
    a1raw = at("a1raw", [P, NA, K * R1], F32, V0)
    B2X = pair("b2x", [P, K, 3 * R2], V0)
    q = [Q0]

    def small(name, shape, dtype=F32):
        size = 4
        for n in shape[1:]:
            size *= n
        t = at(name, shape, dtype, q[0])
        q[0] += -(-size // 32) * 32
        return t

    ident = small("ident", [P, P])
    b2stage = small("b2stage", [SEG2, BANK], F32R)
    idx_a = small("idx_a", [1, B], I32)
    idx_l = small("idx_l", [1, B], I32)
    lang = small("lang", [P, B], I32)
    langf = small("langf", [P, NB])
    iota = small("iota", [P, E])
    bias = small("bias", [P, NB, E])
    lg = small("lg", [P, E])
    top = small("top", [P, 8])
    topi = small("topi", [P, 8], U32)
    topf = small("topf", [P, 2])
    ex = small("ex", [P, 1])
    den = small("den", [P, 1])
    gw = small("gw", [P, 2])
    gm = small("gm", [P, 2, E])
    gate = small("gate", [P, E])
    assert q[0] <= 229344

    q[0] = EY[2]
    XS = (small("xs_hi", [P, K, P], F32R), small("xs_lo", [P, K, P], F32R))
    S = (small("s_hi", [P, K, SC], F32R), small("s_lo", [P, K, SC], F32R))
    assert q[0] <= Z0
    q[0] = EY[0]
    XT = [(small("xt0_hi", [P, K, P], F32R), small("xt0_lo", [P, K, P], F32R))]
    b1s = [small(f"b1s{s}", [2 * SEG1, D + C3 + PER * R2], F32R) for s in range(2)]
    b2s = small("b2s", [SEG2, D + C3], F32R)
    h1c = small("h1c", [P, 2 * SEG1], F32R)
    h1T = small("h1T", [2 * SEG1, P], F32R)
    h2c = small("h2c", [P, 3, R2], F32R)
    h2T = small("h2T", [SEG2, P], F32R)
    gh = small("gh", [P, E, R3])
    GHT = (small("ght_hi", [P, P], F32R), small("ght_lo", [P, P], F32R))
    assert q[0] <= EY[1]
    q[0] = EY[1]
    XT.append((small("xt1_hi", [P, K, P], F32R), small("xt1_lo", [P, K, P], F32R)))
    b3raw = small("b3raw", [P, E, K * R3])
    b3p = small("b3p", [P, K, ER])
    B3 = (small("b3_hi", [P, D], F32R), small("b3_lo", [P, D], F32R))
    assert q[0] <= EY[2]

    with ExitStack() as ctx:
        bank = [ctx.enter_context(nc.psum_tensor(f"bank{n}", [P, BANK], F32)) for n in range(8)]

        def sem(name):
            return ctx.enter_context(nc.semaphore(name))

        b1scr = nc.dram_tensor("b1scr", (NA, 2, R1, XC), F32).ap()
        b2scr = nc.dram_tensor("b2scr", (SEG2, D + C3), F32).ap()

        s_idx = sem("s_idx")
        s_raw = [sem(f"s_raw{n}") for n in range(3)]
        s_free = [sem(f"s_free{n}") for n in range(3)]
        s_early = [sem(f"s_early{n}") for n in range(2)]
        s_w2 = [sem(f"s_w2{k}") for k in range(K)]
        s_w2l = sem("s_w2l")
        s_c3h = sem("s_c3h")
        s_c3l = sem("s_c3l")
        s_b1z = sem("s_b1z")
        s_a2 = [sem(f"s_a2{n}") for n in range(2)]
        s_a1 = sem("s_a1")
        s_id = sem("s_id")
        s_cst = sem("s_cst")
        s_diag = sem("s_diag")
        s_diag1 = sem("s_diag1")
        s_sh = sem("s_sh")
        s_tp = sem("s_tp")
        s_th = sem("s_th")
        s_tl = sem("s_tl")
        s_acc = sem("s_acc")
        s_acch = sem("s_acch")
        s_accl = sem("s_accl")
        s_b2st = sem("s_b2st")
        s_b1st = sem("s_b1st")
        s_bdz = sem("s_bdz")
        s_w0 = [sem(f"s_w0{n}") for n in range(2)]
        s_b1s = [sem(f"s_b1s{n}") for n in range(2)]
        s_b2s = sem("s_b2s")
        s_b3 = sem("s_b3")
        s_b3p = sem("s_b3p")
        s_b3t = sem("s_b3t")
        s_b3h = sem("s_b3h")
        s_b3l = sem("s_b3l")
        s_bd = sem("s_bd")
        s_bdc = sem("s_bdc")
        s_sel = sem("s_sel")
        s_a1c = sem("s_a1c")
        s_z = sem("s_z")
        s_xh = sem("s_xh")
        s_l0 = sem("s_l0")
        s_xth = sem("s_xth")
        s_xtl = sem("s_xtl")
        s_small = sem("s_small")
        s_h1c = sem("s_h1c")
        s_h2c = sem("s_h2c")
        s_ht = sem("s_ht")
        s_hts = sem("s_hts")
        s_ghl = sem("s_ghl")
        s_dc = sem("s_dc")
        s_top = sem("s_top")
        s_ex = sem("s_ex")
        s_gh = sem("s_gh")
        s_y = sem("s_y")
        s_yfree = [sem("s_yfree0"), sem("s_yfree1")]
        s_st = [sem(f"s_st{n}") for n in range(2)]

        w1rows = w1.rearrange("(p k) o -> k p o", k=K)
        b1rows = b1.rearrange("(n a) r o -> n (a r) o", n=LORA)
        W3SEQ = [6, 7, 0, 1, 2, 3, 4, 5]
        assert W3SEQ[:2] == list(range(2 * F3C // P, K))
        TG_W3 = 3
        TG_W1 = TG_W3 + 2 * K
        items = [("a3", 0), ("wr", 0), ("b2", 0)] + [("w3", rb) for rb in W3SEQ[2:]] + [("a2", 2), ("a2", 0)]
        place = {it: n % 3 for n, it in enumerate(items)}
        landed, read_out = {}, {}
        arrived, freed = [0, 0, 0], [0, 0, 0]
        for it in items:
            s = place[it]
            if it[0] != "a2":
                arrived[s] += 1
                landed[it] = (s_raw[s], 16 * arrived[s])
            if it[0] == "w3":
                read_out[it] = (s_tp, TG_W3 + 2 * W3SEQ.index(it[1]) + 2)
            elif it[0] in ("a3", "wr"):
                read_out[it] = (s_tp, {"a3": 2, "wr": 3}[it[0]])
            else:
                freed[s] += 1
                read_out[it] = (s_free[s], freed[s])
        assert (place[items[-2]], place[items[-1]]) == (0, 1)
        RAW_ROWS = arrived[:2]
        XIN = [arrived[s] + ROWS // 2 for s in range(2)]
        XOUT = freed[:2]

        def w3_tile(rb):
            n = W3SEQ.index(rb)
            return (early[n], (s_early[n], 16)) if n < 2 else (raw[place[("w3", rb)]], landed[("w3", rb)])

        def turned_w3(g):
            n, h = divmod(g - TG_W3, 2)
            c, r = divmod(W3SEQ[n], F3C // P)
            return c, slice(4 * h, 4 * h + 4), slice(r * P, (r + 1) * P)

        def four(t):
            return t.rearrange("p (k n) -> p k n", k=4)

        PARTS = {2: ((0, D - 2 * F3C, M, 2 * F3C), (D - 2 * F3C, WIDTH[2], TB, 0)),
                 0: ((0, F3C, M, 0), (F3C, WIDTH[0], TB, WIDTH[2] - (D - 2 * F3C))), 1: ((0, F3C, M, F3C),)}
        OUT = sum(len(parts) for parts in PARTS.values())
        OUT_AT = [2, 4, 5]

        def in_place(b1scr_rows, c):
            runs = [(0, WIDTH[2])] if c == 2 else [(0, F3C)]
            places = [(lo, hi, b1scr_rows[:, :, :, COLUMN[c] + lo:COLUMN[c] + hi]) for lo, hi in runs]
            if c == 0:
                places.append((F3C, WIDTH[0], b1scr_rows[:, :, :, D + A2COL[0]:XC]))
            return places

        BETWEEN = {(0, 6): (7, 8), (0, 7): (9, 10), (0, 8): (11, 12), (1, 1): (13,), (1, 2): (14,), (1, 3): (15,),
                   (1, 4): (16,), (1, 5): (17,), (1, 6): (18,)}
        OUTER = 6
        COLUMN = [0, F3C, 2 * F3C]
        A2COL = {2: C3, 0: C3 + 3 * R2}

        def stage_bank(r, j):
            return bank[3 * (r % 2) + j]

        T_BANK = [bank[6 + (TG_W1 + h) % 2] for h in range(2)]
        L0_BANK = bank[6:8]

        xrows = x.rearrange("(n s) t d -> n (s t) d", s=PER)
        orows = out.rearrange("(n s) t d -> n (s t) d", s=PER)

        block = ctx.enter_context(nc.Block())

        @block.sync
        def _(sp):
            def load(it):
                s, n = place[it], items.index(it)
                if n >= 3:
                    sp.wait_ge(*read_out[items[n - 3]])
                kind, n = it
                if kind == "a2":
                    dst = raw[s][:, 0:3 * K * R2].rearrange("p (l k r) -> p l k r", l=3, k=K)
                    for m, l in enumerate(LABELERS[n]):
                        sp.dma_start(dst[:, m], a2[l].rearrange("(k p) r -> p k r", p=P)).then_inc(s_a2[s], 16)
                    return
                dst = raw[s][:, :]
                if kind == "a3":
                    src = a3.rearrange("e r d -> (e r) d")
                elif kind == "wr":
                    dst, src = raw[s][0:E, :], wr
                elif kind == "b2":
                    dst, src = raw[s][:, 0:K * R2].rearrange("p (k r) -> p k r", k=K), b2.rearrange("(k p) r -> p k r", p=P)
                else:
                    src = w3[n * P:(n + 1) * P, :]
                sp.dma_start(dst, src).then_inc(s_raw[s], 16)

            load(items[0])
            load(items[1])
            for n in range(2):
                rb = W3SEQ[n]
                sp.dma_start(early[n][:, :], w3[rb * P:(rb + 1) * P, :]).then_inc(s_early[n], 16)
            load(items[2])
            for k in range(K):
                sp.dma_start(w2raw[k][:, :], w2[k * P:(k + 1) * P, :]).then_inc(s_w2[k], 16)
            sp.dma_start(idx_a[:, :], idx_adapter.rearrange("(a n) -> a n", a=1)).then_inc(s_idx, 16)
            sp.dma_start(idx_l[:, :], idx_labeler.rearrange("(a n) -> a n", a=1)).then_inc(s_idx, 16)
            sp.dma_start(lang[:, :], idx_language.partition_broadcast(P)).then_inc(s_idx, 16)
            for it in items[3:]:
                load(it)

            def load_rows(r, u, src):
                if isinstance(r, int) and r < 2:
                    sp.wait_ge(*read_out[items[-2 + r]])
                else:
                    sp.wait_ge(s_tp, 2 * r + (TG_W1 - 2))
                sp.dma_start(raw[u][:, :], src).then_inc(s_raw[u], 16)

            def w1_of(r):
                return w1rows[r - LORA] if isinstance(r, int) else w1rows[bass.ds(r - LORA, 1)].rearrange("a p o -> (a p) o")

            def store_lora(r):
                dst = b1scr[r * P // R1:(r + 1) * P // R1]
                for j, c in enumerate(ORDER):
                    sp.wait_ge(s_accl, ACC_A + OUT * r + OUT_AT[j])
                    for lo_, hi_, scr in in_place(dst, c):
                        for half in range(2):
                            sp.dma_start(scr[:, half], f32(b1stage[3 * r + j][half][:, lo_:hi_])).then_inc(s_b1st, 16)

            load_rows(0, 0, b1rows[0])
            load_rows(1, 1, b1rows[1])
            load_rows(2, 0, w1_of(2))
            load_rows(3, 1, w1_of(3))
            sp.wait_ge(s_acc, ACC_A)
            sp.dma_start(a1raw[:, :, :], a1.rearrange("a (p k) r -> p a (k r)", k=K)).then_inc(s_a1, 16)
            store_lora(0)
            load_rows(4, 0, w1_of(4))
            load_rows(5, 1, w1_of(5))
            store_lora(1)
            with sp.Fori(3, ROWS // 2) as i:
                for u in range(2):
                    load_rows(2 * i + u, u, w1_of(2 * i + u))

            sp.wait_ge(s_idx, 48)

            def index(tile, n, count):
                return sp.value_load(tile[0:1, bass.ds(n, 1)], min_val=0, max_val=count - 1)

            def load_w0(b, s):
                for h in range(PER):
                    a = index(idx_a, PER * b + h, NA)
                    sp.dma_start(bdraw[s][h * T:(h + 1) * T, h * T:(h + 1) * T],
                                 w0[bass.ds(a, 1)].rearrange("a c d -> (a c) d")).then_inc(s_w0[s], 16)

            def load_b1s(b, s):
                for h in range(PER):
                    a = index(idx_a, PER * b + h, NA)
                    lab = index(idx_l, PER * b + h, NL)
                    both, again = slice(h * SEG1, h * SEG1 + 2 * R1), slice(h * SEG1 + 2 * R1, (h + 1) * SEG1)
                    for rows, halves in ((both, slice(0, 2)), (again, slice(0, 1))):
                        for cols, scr_cols in ((slice(0, D + C3), slice(0, D + C3)),
                                               (slice(D + C3 + h * R2, D + C3 + (h + 1) * R2), bass.ds(lab * R2 + (D + C3), R2))):
                            sp.dma_start(f32(b1s[s][rows, cols]),
                                         b1scr[bass.ds(a, 1), halves, :, scr_cols].rearrange("a s r c -> (a s r) c")
                                         ).then_inc(s_b1s[s], 16)

            sp.wait_ge(s_bdz, 2)
            load_w0(0, 0)
            load_w0(1, 1)
            for b in range(2):
                load_rows(ROWS + b, b, xrows[b])
            sp.wait_ge(s_b1st, 16 * 8 * LORA)
            sp.wait_ge(s_b2st, 16 * 3)
            sp.wait_ge(s_acc, ACC_A + ACC_B - 1)
            sp.wait_ge(s_b1z, 2)
            load_b1s(0, 0)
            sp.dma_start(f32(b2s[:, :]), b2scr).then_inc(s_b2s, 16)
            sp.wait_ge(s_acc, ACC_A + ACC_B)
            sp.dma_start(b3raw[:, :, :], b3.rearrange("e (p k) r -> p e (k r)", k=K)).then_inc(s_b3, 16)
            load_b1s(1, 1)

            def block_io(i, s, last):
                b = 2 * i + s
                if not last:
                    sp.wait_ge(s_free[s], i + XOUT[s] + 1)
                    sp.dma_start(raw[s][:, :], xrows[bass.ds(b + 2, 1)].rearrange("a t d -> (a t) d")).then_inc(s_raw[s], 16)
                    sp.wait_ge(s_bd, b + 1)
                    load_w0(b + 2, s)
                sp.wait_ge(s_yfree[0], b + 1)
                sp.wait_ge(s_yfree[1], b + 1)
                if last:
                    sp.dma_start(orows[b], ost[s][:, :]).then_inc(s_st[s], 16)
                else:
                    sp.dma_start(orows[bass.ds(b, 1)].rearrange("a t d -> (a t) d"), ost[s][:, :]).then_inc(s_st[s], 16)
                if not last:
                    load_b1s(b + 2, s)

            for s in range(2):
                block_io(0, s, False)
            with sp.Fori(1, NB // 2 - 1) as i:
                for s in range(2):
                    block_io(i, s, False)
            for s in range(2):
                block_io(NB // 2 - 1, s, True)
            for s in range(2):
                sp.wait_ge(s_st[s], 16 * (NB // 2))

        @block.gpsimd
        def _(pool):
            nc.gpsimd.memset(ident[:, :], 0.0).then_inc(s_id, 1)
            pool.wait_ge(s_id, 1)
            nc.gpsimd.affine_select(out=ident[:, :], in_=ident[:, :], compare_op=ALU.not_equal, fill=1.0,
                                    base=0, pattern=[[-1, P]], channel_multiplier=1).then_inc(s_id, 1)
            pool.wait_ge(s_id, 2)

            def add_identity(tile, landed_at, n):
                pool.wait_ge(*landed_at)
                blk = tile[:, n * P:(n + 1) * P]
                nc.gpsimd.tensor_tensor(blk, blk, ident[:, :], ALU.add).then_inc(s_diag, 1)

            def store_b2(m):
                c = ORDER[m]
                pool.wait_ge(s_accl, (K + 1) * (m + 1))
                pool.dma_start(b2scr[:, COLUMN[c]:COLUMN[c] + WIDTH_A[c]], f32(b2stage[:, 0:WIDTH_A[c]])).then_inc(s_b2st, 16)

            for rb in W3SEQ[:2]:
                add_identity(*w3_tile(rb), rb)
            for k in range(K):
                add_identity(w2raw[k], (s_w2[k], 16), k)
            for rb in W3SEQ[2:6]:
                add_identity(*w3_tile(rb), rb)
            store_b2(0)
            for rb in W3SEQ[6:]:
                add_identity(*w3_tile(rb), rb)
            store_b2(1)
            pool.wait_ge(s_tp, TG_W1)
            for s in range(2):
                nc.gpsimd.memset(bdraw[s][:, :], 0.0).then_inc(s_bdz, 1)
            store_b2(2)

            def diagonal(i, s):
                b = 2 * i + s
                pool.wait_ge(s_w0[s], 32 * i + 32)
                nc.gpsimd.tensor_tensor(bdraw[s][:, :], bdraw[s][:, :], ident[:, :], ALU.add).then_inc(s_bdc, 1)
                there, free = held(pool, 2 * b + 1), held(pool, 2 * b)
                pool.wait_ge(s_id, 2)
                above(pool, s_l0, free)
                pool.wait_ge(s_bdc, there)
                nc.gpsimd.tensor_copy(BD[0][:, :], bdraw[s][:, :]).then_inc(s_bdc, 1)
                pool.wait_ge(s_bdc, 2 * b + 2)
                nc.gpsimd.tensor_tensor(BD[1][:, :], bdraw[s][:, :], f32(BD[0][:, :]), ALU.subtract).then_inc(s_bd, 1)

            def select(b):
                a = [pool.value_load(idx_a[0:1, bass.ds(PER * b + h, 1)], min_val=0, max_val=NA - 1) for h in range(PER)]
                l = [pool.value_load(idx_l[0:1, bass.ds(PER * b + h, 1)], min_val=0, max_val=NL - 1) for h in range(PER)]
                a1_of = [a1raw[:, bass.ds(n, 1), :].rearrange("p a (k r) -> p (a k) r", k=K) for n in a]
                free, there = held(pool, 3 * b - 2), held(pool, 2 * b + 2)
                pool.wait_ge(s_id, 2)
                above(pool, s_small, free)
                for h in range(PER):
                    at_ = C3 + PER * R2 + h * R1
                    nc.gpsimd.tensor_copy(S[0][:, :, at_:at_ + R1], a1_of[h]).then_inc(s_a1c, 1)
                for h in range(PER):
                    at_ = C3 + h * R2
                    for z in range(2):
                        nc.gpsimd.tensor_copy(S[z][:, :, at_:at_ + R2],
                                              f32(TB[z])[:, :, bass.ds(l[h] * R2 + C3, R2)]).then_inc(s_sel, 1)
                pool.wait_ge(s_id, 2)
                pool.wait_ge(s_a1c, there)
                for h in range(PER):
                    at_ = C3 + PER * R2 + h * R1
                    nc.gpsimd.tensor_tensor(S[1][:, :, at_:at_ + R1], a1_of[h], f32(S[0][:, :, at_:at_ + R1]),
                                            ALU.subtract).then_inc(s_sel, 1)

            pool.wait_ge(s_idx, 48)
            pool.wait_ge(s_bdz, 2)
            diagonal(0, 0)
            pool.wait_ge(s_a1, 16)
            pool.wait_ge(s_acc, ACC_A + ACC_B - 1)
            for s in range(2):
                nc.gpsimd.memset(f32(b1s[s][:, D + C3:]), 0.0).then_inc(s_b1z, 1)
            pool.wait_ge(s_accl, ACC_A + OUT * (ROWS - 1) + OUT_AT[1])
            select(0)
            diagonal(0, 1)
            pool.wait_ge(s_b3, 16)
            nc.gpsimd.tensor_copy(b3p[:, :, :].rearrange("p k (e r) -> p k e r", e=E),
                                  b3raw[:, :, :].rearrange("p e (k r) -> p k e r", k=K)).then_inc(s_b3p, 1)
            select(1)
            diagonal(1, 0)
            select(2)
            diagonal(1, 1)
            with pool.Fori(1, NB // 2 - 1) as i:
                select(2 * i + 1)
                diagonal(i + 1, 0)
                select(2 * i + 2)
                diagonal(i + 1, 1)
            select(NB - 1)

        @block.scalar
        def _(act):
            def split_hi(dst, src, landed_at):
                act.wait_ge(*landed_at)
                nc.scalar.activation(dst, src, ACT.Copy).then_inc(s_sh, 1)

            def turn_hi(g, dst, src):
                act.wait_ge(s_tp, g + 1)
                nc.scalar.activation(dst, src, ACT.Copy).then_inc(s_th, 1)

            def turn_w3(g):
                c, ks, cs = turned_w3(g)
                turn_hi(g, G[c][0][:, ks, cs], four(bank[6 + g % 2]))

            def turn_rows(r, u):
                for h in range(2):
                    if h == 0 and not (isinstance(r, int) and r == 0):
                        act.wait_ge(s_acc, ACC_A + 3 * (r - 1))
                    act.wait_ge(s_tp, 2 * r + (TG_W1 + h + 1))
                    nc.scalar.activation(W1T[u][0][:, 4 * h:4 * h + 4, :], four(T_BANK[h]), ACT.Copy).then_inc(s_th, 1)

            for g in range(2):
                turn_hi(g, G[2][0][:, 4 * g:4 * g + 4, D - 2 * F3C:D - 2 * F3C + ER], four(bank[6 + g % 2]))
            turn_hi(2, G[2][0][:, :, D - 2 * F3C + ER:], bank[6][:, 0:K * E].rearrange("p (k n) -> p k n", k=K))
            for g in range(TG_W3, TG_W3 + 4):
                turn_w3(g)
            s = place[("b2", 0)]
            split_hi(B2X[0][:, :, :].rearrange("p k (m r) -> p k m r", m=3),
                     raw[s][:, 0:K * R2].rearrange("p (k m r) -> p k m r", k=K, m=1).to_broadcast([P, K, 3, R2]),
                     landed[("b2", 0)])
            for k in range(K):
                split_hi(W2S[0][:, k, :], w2raw[k][:, :], (s_diag, 2 + k + 1))
            n = 0
            for m, c in enumerate(ORDER):
                w = WIDTH_A[c]
                for ob in range(K + 1):
                    for g in BETWEEN.get((m, ob), ()):
                        turn_w3(g)
                    if m == 2 and ob in (1, 2):
                        part = ORDER[ob - 1]
                        s, count, at_ = place[("a2", part)], len(LABELERS[part]), WIDTH_A[part]
                        act.wait_ge(s_a2[s], 16 * count)
                        nc.scalar.activation(EX[part][0][:, :, at_:].rearrange("p k (l r) -> p l k r", r=R2),
                                             raw[s][:, 0:count * K * R2].rearrange("p (l k r) -> p l k r", k=K, r=R2),
                                             ACT.Copy).then_inc(s_sh, 1)
                    if m == 2 and ob == K:
                        turn_rows(0, 0)
                    if ob == K and m > 0:
                        act.wait_ge(s_b2st, 16 * m)
                    act.wait_ge(s_acc, n + 1)
                    if ob < K:
                        nc.scalar.activation(EX[c][0][:, ob, 0:w], bank[n % 6][:, 0:w], ACT.Copy).then_inc(s_acch, 1)
                    else:
                        nc.scalar.activation(b2stage[:, 0:w], bank[n % 6][0:SEG2, 0:w], ACT.Copy).then_inc(s_acch, 1)
                    n += 1

            def rows_hi(r, u, chunks=range(3)):
                for j in chunks:
                    act.wait_ge(s_id, 2)
                    act.wait_ge(s_acc, 3 * r + (ACC_A + j + 1))
                    for lo_, hi_, dst, at_ in PARTS[ORDER[j]]:
                        src = stage_bank(u, j)[:, lo_:hi_]
                        if isinstance(r, int) and r < LORA:
                            out_ = b1stage[3 * r + j][0][:, lo_:hi_]
                        else:
                            out_ = dst[0][:, bass.ds(r - LORA, 1), at_:at_ + hi_ - lo_].rearrange("p a n -> p (a n)")
                        nc.scalar.activation(out_, src, ACT.Copy).then_inc(s_acch, 1)

            turn_rows(1, 1)
            rows_hi(0, 0)
            turn_rows(2, 0)
            rows_hi(1, 1)
            with act.Fori(1, ROWS // 2 - 1) as i:
                turn_rows(2 * i + 1, 1)
                rows_hi(2 * i, 0)
                turn_rows(2 * i + 2, 0)
                act.wait_ge(s_b1st, 16 * 8 * LORA)
                rows_hi(2 * i + 1, 1)
            turn_rows(ROWS - 1, 1)
            rows_hi(ROWS - 2, 0)

            def x_hi(i, s):
                b = 2 * i + s
                act.wait_ge(s_raw[s], 16 * i + 16 * (XIN[s] + 1))
                above(act, s_l0, 2 * b)
                nc.scalar.activation(XS[0][:, :, :], raw[s].rearrange("t (p k) -> t k p", k=K), ACT.Copy).then_inc(s_xh, 1)

            def xt_hi(b, s):
                for h in range(2):
                    act.wait_ge(s_l0, 2 * b + h + 1)
                    nc.scalar.activation(XT[s][0][:, 4 * h:4 * h + 4, :], four(L0_BANK[h]), ACT.Copy).then_inc(s_xth, 1)

            def block_hi(i, s, last):
                b = 2 * i + s
                t = bank[5]
                if not last:
                    x_hi(i + s, 1 - s)
                act.wait_ge(s_ht, 3 * b + 1)
                nc.scalar.activation(h1T[:, :], t[0:2 * SEG1, 0:P], ACT.Copy).then_inc(s_hts, 1)
                if not last:
                    above(act, s_y, 2 * b)
                    xt_hi(b + 1, 1 - s)
                if isinstance(b, int) and b == 0:
                    for h in range(2):
                        act.wait_ge(s_b3t, h + 1)
                        nc.scalar.activation(B3[0].rearrange("q (p k) -> q k p", k=K)[:, 4 * h:4 * h + 4, :],
                                             four(bank[2 + h]), ACT.Copy).then_inc(s_b3h, 1)
                act.wait_ge(s_ht, 3 * b + 2)
                nc.scalar.activation(h2T[:, :], t[0:SEG2, P:2 * P], ACT.Copy).then_inc(s_hts, 1)
                act.wait_ge(s_top, b + 1)
                nc.scalar.activation(ex[:, :], top[:, 0:1], ACT.Exp, bias=top[:, 1:2], scale=-1.0).then_inc(s_ex, 1)
                act.wait_ge(s_ht, 3 * b + 3)
                nc.scalar.activation(GHT[0][:, :], t[:, 2 * P:3 * P], ACT.Copy).then_inc(s_hts, 1)
                act.wait_ge(s_y, 2 * b + 1)
                above(act, s_st[s], 16 * i)
                nc.scalar.activation(ost[s][:, 0:BANK], bank[2 * s][:, :], ACT.Copy).then_inc(s_yfree[0], 1)

            rows_hi(ROWS - 1, 1, [0])
            x_hi(0, 0)
            act.wait_ge(s_acch, ACC_A + OUT * (ROWS - 1) + OUT_AT[0])
            nc.scalar.activation(S[0][:, :, 0:C3], f32(TB[0])[:, :, 0:C3], ACT.Copy).then_inc(s_c3h, 1)
            rows_hi(ROWS - 1, 1, [1])
            xt_hi(0, 0)
            rows_hi(ROWS - 1, 1, [2])
            for s in range(2):
                block_hi(0, s, False)
            with act.Fori(1, NB // 2 - 1) as i:
                for s in range(2):
                    block_hi(i, s, False)
            block_hi(NB // 2 - 1, 0, False)
            block_hi(NB // 2 - 1, 1, True)

        @block.vector
        def _(dve):
            V = nc.vector

            def lo(dst, src, hi, signal):
                V.tensor_tensor(dst, src, f32(hi), ALU.subtract).then_inc(signal, 1)

            def turn_lo(g, dst, hi, src):
                dve.wait_ge(s_th, g + 1)
                lo(dst, src, hi, s_tl)

            def turn_w3(g):
                c, ks, cs = turned_w3(g)
                turn_lo(g, G[c][1][:, ks, cs], G[c][0][:, ks, cs], four(bank[6 + g % 2]))

            def turn_rows(r, u):
                for h in range(2):
                    ks = slice(4 * h, 4 * h + 4)
                    dve.wait_ge(s_th, 2 * r + (TG_W1 + h + 1))
                    lo(W1T[u][1][:, ks, :], four(T_BANK[h]), W1T[u][0][:, ks, :], s_tl)

            for g in range(2):
                part = (slice(None), slice(4 * g, 4 * g + 4), slice(D - 2 * F3C, D - 2 * F3C + ER))
                turn_lo(g, G[2][1][part], G[2][0][part], four(bank[6 + g % 2]))
            part = (slice(None), slice(None), slice(D - 2 * F3C + ER, None))
            turn_lo(2, G[2][1][part], G[2][0][part], bank[6][:, 0:K * E].rearrange("p (k n) -> p k n", k=K))
            for g in range(TG_W3, TG_W3 + 4):
                turn_w3(g)
            s = place[("b2", 0)]
            dve.wait_ge(s_sh, 1)
            V.tensor_tensor(B2X[1][:, :, :].rearrange("p k (m r) -> p k m r", m=3),
                            raw[s][:, 0:K * R2].rearrange("p (k m r) -> p k m r", k=K, m=1).to_broadcast([P, K, 3, R2]),
                            f32(B2X[0][:, :, :]).rearrange("p k (m r) -> p k m r", m=3), ALU.subtract).then_inc(s_free[s], 1)
            for k in range(K):
                dve.wait_ge(s_sh, k + 2)
                lo(W2S[1][:, k, :], w2raw[k][:, :], W2S[0][:, k, :], s_w2l)
            n = 0
            for m, c in enumerate(ORDER):
                w = WIDTH_A[c]
                for ob in range(K + 1):
                    for g in BETWEEN.get((m, ob), ()):
                        turn_w3(g)
                    if m == 2 and ob in (1, 2):
                        part = ORDER[ob - 1]
                        s, count, at_ = place[("a2", part)], len(LABELERS[part]), WIDTH_A[part]
                        dve.wait_ge(s_sh, 1 + K + ob)
                        lo(EX[part][1][:, :, at_:].rearrange("p k (l r) -> p l k r", r=R2),
                           raw[s][:, 0:count * K * R2].rearrange("p (l k r) -> p l k r", k=K, r=R2),
                           EX[part][0][:, :, at_:].rearrange("p k (l r) -> p l k r", r=R2), s_free[s])
                    if m == 2 and ob == K:
                        turn_rows(0, 0)
                    dve.wait_ge(s_acch, n + 1)
                    if ob < K:
                        lo(EX[c][1][:, ob, 0:w], bank[n % 6][:, 0:w], EX[c][0][:, ob, 0:w], s_accl)
                    else:
                        mid = slice(R2, 2 * R2)
                        lo(b2stage[mid, 0:w], bank[n % 6][mid, 0:w], b2stage[mid, 0:w], s_accl)
                    n += 1

            def identity_rows(r, u):
                dve.wait_ge(s_raw[u], 8 * r + (16 * (RAW_ROWS[u] + 1) - 8 * u))
                blk = raw[u].rearrange("q (p k) -> q k p", k=K)[:, bass.ds(r - LORA, 1), :].rearrange("q a p -> q (a p)")
                V.tensor_tensor(blk, blk, ident[:, :], ALU.add).then_inc(s_diag1, 1)

            def rows_lo(r, u, chunks=range(3)):
                for j in chunks:
                    dve.wait_ge(s_acch, OUT * r + (ACC_A + OUT_AT[j]))
                    for lo_, hi_, dst, at_ in PARTS[ORDER[j]]:
                        if isinstance(r, int) and r < LORA:
                            hi, out_ = [b1stage[3 * r + j][z][:, lo_:hi_] for z in range(2)]
                        else:
                            hi, out_ = [dst[z][:, bass.ds(r - LORA, 1), at_:at_ + hi_ - lo_].rearrange("p a n -> p (a n)")
                                        for z in range(2)]
                        lo(out_, stage_bank(u, j)[:, lo_:hi_], hi, s_accl)

            dve.wait_ge(s_id, 2)
            turn_rows(1, 1)
            identity_rows(2, 0)
            rows_lo(0, 0)
            turn_rows(2, 0)
            identity_rows(3, 1)
            rows_lo(1, 1)
            for e in range(E):
                V.memset(iota[:, e:e + 1], float(e)).then_inc(s_cst, 1)
            dve.wait_ge(s_idx, 48)
            for h in range(PER):
                ts = slice(h * T, (h + 1) * T)
                V.tensor_copy(langf[ts, :], lang[ts, :].rearrange("p (t h) -> p h t", h=PER)[:, h, :]).then_inc(s_cst, 1)
            dve.wait_ge(s_cst, E + 2)
            V.tensor_tensor(bias[:, :, :], langf[:, :].unsqueeze(2).to_broadcast([P, NB, E]),
                            iota[:, :].unsqueeze(1).to_broadcast([P, NB, E]), ALU.is_equal).then_inc(s_cst, 1)
            dve.wait_ge(s_cst, E + 3)
            V.tensor_scalar(bias[:, :, :], bias[:, :, :], LANG_BIAS, None, ALU.mult).then_inc(s_cst, 1)
            with dve.Fori(1, ROWS // 2 - 1) as i:
                turn_rows(2 * i + 1, 1)
                identity_rows(2 * i + 2, 0)
                rows_lo(2 * i, 0)
                turn_rows(2 * i + 2, 0)
                identity_rows(2 * i + 3, 1)
                rows_lo(2 * i + 1, 1)
            turn_rows(ROWS - 1, 1)
            rows_lo(ROWS - 2, 0)

            def x_lo(b_half, s):
                dve.wait_ge(s_xh, 2 * b_half + s + 1)
                lo(XS[1][:, :, :], raw[s].rearrange("t (p k) -> t k p", k=K), XS[0][:, :, :], s_free[s])

            def xt_lo(b, s):
                for h in range(2):
                    dve.wait_ge(s_xth, 2 * b + h + 1)
                    ks = slice(4 * h, 4 * h + 4)
                    lo(XT[s][1][:, ks, :], four(L0_BANK[h]), XT[s][0][:, ks, :], s_xtl)

            STEPS = 13

            def block_lo(i, s, last):
                b = 2 * i + s
                nar = bank[4]
                done = [0]

                def then(ins):
                    ins.then_inc(s_dc, 1)
                    done[0] += 1

                def hold():
                    dve.wait_ge(s_dc, STEPS * b + done[0])

                if not last:
                    x_lo(i + s, 1 - s)
                dve.wait_ge(s_small, 3 * b + 1)
                for h in range(PER):
                    ts, at_ = slice(h * T, (h + 1) * T), C3 + PER * R2 + h * R1
                    then(V.tensor_copy(h1c[ts, h * SEG1:h * SEG1 + 2 * R1].rearrange("p (m r) -> p m r", m=2),
                                       nar[ts, at_:at_ + R1].unsqueeze(1).to_broadcast([T, 2, R1])))
                hold()
                for h in range(PER):
                    ts, at_ = slice(h * T, (h + 1) * T), C3 + PER * R2 + h * R1
                    lo(h1c[ts, h * SEG1 + 2 * R1:(h + 1) * SEG1], nar[ts, at_:at_ + R1], h1c[ts, h * SEG1:h * SEG1 + R1], s_h1c)
                if not last:
                    xt_lo(b + 1, 1 - s)
                if isinstance(b, int) and b == 0:
                    for h in range(2):
                        dve.wait_ge(s_b3h, h + 1)
                        dst, hi = [B3[z].rearrange("q (p k) -> q k p", k=K)[:, 4 * h:4 * h + 4, :] for z in (1, 0)]
                        lo(dst, four(bank[2 + h]), hi, s_b3l)
                dve.wait_ge(s_small, 3 * b + 2)
                for h in range(PER):
                    ts, at_ = slice(h * T, (h + 1) * T), C3 + h * R2
                    then(V.tensor_scalar(h2c[ts, 0:2, :], nar[ts, at_:at_ + R2].unsqueeze(1).to_broadcast([T, 2, R2]),
                                         SCALE2, None, ALU.mult))
                hold()
                for h in range(PER):
                    ts, at_ = slice(h * T, (h + 1) * T), C3 + h * R2
                    V.scalar_tensor_tensor(h2c[ts, 2, :], nar[ts, at_:at_ + R2], SCALE2, f32(h2c[ts, 0, :]),
                                           ALU.mult, ALU.subtract).then_inc(s_h2c, 1)
                dve.wait_ge(s_small, 3 * b + 3)
                then(V.tensor_tensor(lg[:, :], nar[:, ER:C3], bias[:, bass.ds(b, 1), :].rearrange("p a e -> p (a e)"), ALU.add))
                logits_there = held(dve, STEPS * b + done[0])
                dve.wait_ge(s_id, 2)
                dve.wait_ge(s_dc, logits_there)
                V.max(top[:, :], lg[:, :]).then_inc(s_top, 1)
                dve.wait_ge(s_id, 2)
                dve.wait_ge(s_top, b + 1)
                then(V.max_index(topi[:, :], top[:, :], lg[:, :]))
                hold()
                then(V.tensor_copy(topf[:, :], topi[:, 0:2]))
                dve.wait_ge(s_ex, b + 1)
                then(V.tensor_scalar(den[:, :], ex[:, :], 1.0, 1.0 / SCALE3, ALU.add, ALU.mult))
                hold()
                then(V.reciprocal(gw[:, 0:1], den[:, :]))
                hold()
                then(V.tensor_tensor(gw[:, 1:2], gw[:, 0:1], ex[:, :], ALU.mult))
                hold()
                for m in range(2):
                    then(V.tensor_scalar(gm[:, m, :], iota[:, :], topf[:, m:m + 1], gw[:, m:m + 1], ALU.is_equal, ALU.mult))
                hold()
                then(V.tensor_tensor(gate[:, :], gm[:, 0, :], gm[:, 1, :], ALU.add))
                hold()
                V.tensor_tensor(gh[:, :, :], nar[:, 0:ER].rearrange("p (e r) -> p e r", e=E),
                                gate[:, :].unsqueeze(2).to_broadcast([P, E, R3]), ALU.mult).then_inc(s_gh, 1)
                assert done[0] == STEPS, done
                dve.wait_ge(s_hts, 3 * b + 3)
                lo(GHT[1][:, :], bank[5][:, 2 * P:3 * P], GHT[0][:, :], s_ghl)
                dve.wait_ge(s_y, 2 * b + 2)
                above(dve, s_st[s], 16 * i)
                V.tensor_copy(ost[s][:, BANK:], bank[2 * s + 1][:, :]).then_inc(s_yfree[1], 1)

            rows_lo(ROWS - 1, 1, [0])
            x_lo(0, 0)
            dve.wait_ge(s_accl, ACC_A + OUT * (ROWS - 1) + OUT_AT[0])
            V.tensor_copy(S[1][:, :, 0:C3], f32(TB[1])[:, :, 0:C3]).then_inc(s_c3l, 1)
            rows_lo(ROWS - 1, 1, [1])
            V.memset(f32(h1c[:, :]), 0.0).then_inc(s_z, 1)
            xt_lo(0, 0)
            rows_lo(ROWS - 1, 1, [2])
            dve.wait_ge(s_z, 1)
            dve.wait_ge(s_cst, E + 4)
            for s in range(2):
                block_lo(0, s, False)
            with dve.Fori(1, NB // 2 - 1) as i:
                for s in range(2):
                    block_lo(i, s, False)
            block_lo(NB // 2 - 1, 0, False)
            block_lo(NB // 2 - 1, 1, True)

        @block.tensor
        def _(pe):
            TERMS = ((0, 0), (0, 1), (1, 0))

            def turn(to, source, h, signal):
                for k in range(4):
                    ins = nc.tensor.transpose(to[:, k * P:(k + 1) * P], source[:, (4 * h + k) * P:(4 * h + k + 1) * P], ident[:, :])
                ins.then_inc(signal, 1)

            def turn_w3(g):
                n, h = divmod(g - TG_W3, 2)
                pe.wait_ge(s_tl, g - 1)
                pe.wait_ge(s_diag, n + 1 if n < 2 else K + n + 1)
                turn(bank[6 + g % 2], w3_tile(W3SEQ[n])[0], h, s_tp)

            def turn_rows(r, u):
                for h in range(2):
                    pe.wait_ge(s_tl, 2 * r + (TG_W1 + h - 1))
                    if h == 0 and isinstance(r, int) and r < LORA:
                        pe.wait_ge(s_raw[u], 16 * (RAW_ROWS[u] + r // 2 + 1))
                    elif h == 0:
                        pe.wait_ge(s_diag1, r - LORA + 1)
                    turn(T_BANK[h], raw[u], h, s_tp)

            pe.wait_ge(s_id, 2)
            pe.wait_ge(*landed[("a3", 0)])
            for g in range(2):
                turn(bank[6 + g], raw[place[("a3", 0)]], g, s_tp)
            pe.wait_ge(*landed[("wr", 0)])
            pe.wait_ge(s_tl, 1)
            for k in range(K):
                ins = nc.tensor.transpose(bank[6][:, k * E:(k + 1) * E], raw[place[("wr", 0)]][0:E, k * P:(k + 1) * P],
                                          ident[0:E, 0:E])
            ins.then_inc(s_tp, 1)
            for g in range(TG_W3, TG_W3 + 4):
                turn_w3(g)

            def product(to, ob, c, ks):
                w, rows = WIDTH_A[c], slice(0, P if ob < K else SEG2)
                for k in ks:
                    for a, z in TERMS:
                        lhs = W2S[a][:, k, ob * P:(ob + 1) * P] if ob < K else B2X[a][:, k, :]
                        ins = nc.tensor.matmul(to[rows, 0:w], lhs, G[c][z][:, k, 0:w], start=(k == 0 and (a, z) == TERMS[0]),
                                               stop=(k == K - 1 and (a, z) == TERMS[-1]), skip_group_check=True)
                return ins

            pe.wait_ge(s_tl, TG_W3 + 4)
            for k in range(K):
                pe.wait_ge(s_w2l, k + 1)
                for ob in range(OUTER):
                    ins = product(bank[ob], ob, ORDER[0], [k])
                    if k == K - 1:
                        ins.then_inc(s_acc, 1)
            n = OUTER
            for m, c in enumerate(ORDER):
                for ob in range(OUTER if m == 0 else 0, K + 1):
                    for g in BETWEEN.get((m, ob), ()):
                        turn_w3(g)
                    if m > 0 and ob == 0:
                        pe.wait_ge(s_tl, (0, TG_W3 + 10, TG_W1)[m])
                    if m == 2 and ob == K:
                        turn_rows(0, 0)
                    if m == 0 and ob == K:
                        pe.wait_ge(*read_out[("b2", 0)])
                    pe.wait_ge(s_accl, n - 5)
                    product(bank[n % 6], ob, c, range(K)).then_inc(s_acc, 1)
                    n += 1

            def rows(r, u, chunks=range(3)):
                first_row = isinstance(r, int) and r == 0
                for j in chunks:
                    c = ORDER[j]
                    if j == 0:
                        pe.wait_ge(s_tl, 2 * r + (TG_W1 + 2))
                    if first_row:
                        pe.wait_ge(s_accl, ACC_A - 2 + j)
                    elif not (isinstance(r, int) and r == 1):
                        pe.wait_ge(s_accl, OUT * r + (ACC_A - 2 * OUT + OUT_AT[j]))
                    for k in range(K):
                        for a, z in TERMS:
                            ins = nc.tensor.matmul(stage_bank(u, j)[:, 0:WIDTH[c]], W1T[u][a][:, k, :], EX[c][z][:, k, :],
                                                   start=(k == 0 and (a, z) == TERMS[0]), stop=(k == K - 1 and (a, z) == TERMS[-1]))
                    ins.then_inc(s_acc, 1)

            turn_rows(1, 1)
            for it in items[-2:]:
                pe.wait_ge(*read_out[it])
            rows(0, 0)
            turn_rows(2, 0)
            rows(1, 1)
            with pe.Fori(1, ROWS // 2 - 1) as i:
                turn_rows(2 * i + 1, 1)
                rows(2 * i, 0)
                turn_rows(2 * i + 2, 0)
                rows(2 * i + 1, 1)
            turn_rows(ROWS - 1, 1)
            rows(ROWS - 2, 0)

            def layer0(i, s):
                b = 2 * i + s
                pe.wait_ge(s_free[s], i + XOUT[s] + 1)
                pe.wait_ge(s_bd, b + 1)
                above(pe, s_xtl, 2 * b)
                for h in range(2):
                    for k in range(4):
                        for a, z in TERMS:
                            ins = nc.tensor.matmul(L0_BANK[h][:, k * P:(k + 1) * P], XS[a][:, 4 * h + k, :], BD[z][:, :],
                                                   start=(a, z) == TERMS[0], stop=(a, z) == TERMS[-1])
                    ins.then_inc(s_l0, 1)

            def block_products(i, s, last):
                b = 2 * i + s
                first = isinstance(b, int) and b == 0
                nar, t = bank[4], bank[5]
                xt = XT[s]
                pe.wait_ge(s_xtl, 2 * b + 2)
                pe.wait_ge(s_sel, 6 * b + 6)
                above(pe, s_gh, b)
                for k in range(K):
                    for a, z in TERMS:
                        ins = nc.tensor.matmul(nar[:, 0:SC], xt[a][:, k, :], S[z][:, k, :], start=(k == 0 and (a, z) == TERMS[0]),
                                               stop=(k == K - 1 and (a, z) == TERMS[-1]), skip_group_check=True)
                ins.then_inc(s_small, 1)
                if not last:
                    layer0(i + s, 1 - s)
                if first:
                    pe.wait_ge(s_accl, ACC_A + OUT * ROWS)
                    pe.wait_ge(s_b3p, 1)
                    for h in range(2):
                        for k in range(4):
                            ins = nc.tensor.transpose(bank[2 + h][:, k * P:(k + 1) * P], b3p[:, 4 * h + k, :], ident[:, :])
                        ins.then_inc(s_b3t, 1)
                wide = [(c, k, a, z) for k in range(K) for a, z in TERMS for c in range(2)]

                def run(lo_, hi_):
                    for c, k, a, z in wide[lo_:hi_]:
                        nc.tensor.matmul(bank[2 * s + c][:, :], xt[a][:, k, :], M[z][:, k, c * BANK:(c + 1) * BANK],
                                         start=(k == 0 and (a, z) == TERMS[0]), stop=False, skip_group_check=True)

                above(pe, s_yfree[0], b - 1)
                above(pe, s_yfree[1], b - 1)
                run(0, 2)
                pe.wait_ge(s_h1c, 2 * b + 2)
                above(pe, s_ghl, b)
                nc.tensor.transpose(t[0:2 * SEG1, 0:P], f32(h1c[:, :]), ident[:, :]).then_inc(s_ht, 1)
                run(2, 9)
                pe.wait_ge(s_hts, 3 * b + 1)
                pe.wait_ge(s_b1s[s], 128 * i + 128)
                nc.tensor.matmul(nar[:, 0:C3 + PER * R2], h1T[:, :], b1s[s][:, D:], start=False, stop=True,
                                 skip_group_check=True).then_inc(s_small, 1)
                run(9, 16)
                pe.wait_ge(s_h2c, 2 * b + 2)
                nc.tensor.transpose(t[0:SEG2, P:2 * P], f32(h2c[:, :, :]).rearrange("p m r -> p (m r)"), ident[:, :]).then_inc(s_ht, 1)
                run(16, 21)
                pe.wait_ge(s_hts, 3 * b + 2)
                if first:
                    pe.wait_ge(s_b2s, 16)
                nc.tensor.matmul(nar[:, 0:C3], h2T[:, :], b2s[:, D:D + C3], start=False, stop=True,
                                 skip_group_check=True).then_inc(s_small, 1)
                run(21, 44)
                pe.wait_ge(s_gh, b + 1)
                nc.tensor.transpose(t[:, 2 * P:3 * P], gh[:, :, :].rearrange("p e r -> p (e r)"), ident[:, :]).then_inc(s_ht, 1)
                run(44, 48)
                for c in range(2):
                    cols = slice(c * BANK, (c + 1) * BANK)
                    nc.tensor.matmul(bank[2 * s + c][:, :], h1T[:, :], b1s[s][:, cols], start=False, stop=False, skip_group_check=True)
                    nc.tensor.matmul(bank[2 * s + c][:, :], h2T[:, :], b2s[:, cols], start=False, stop=False, skip_group_check=True)
                pe.wait_ge(s_ghl, b + 1)
                if first:
                    pe.wait_ge(s_b3l, 2)
                for c in range(2):
                    cols = slice(c * BANK, (c + 1) * BANK)
                    for a, z in TERMS:
                        ins = nc.tensor.matmul(bank[2 * s + c][:, :], GHT[a][:, :], B3[z][:, cols], start=False,
                                               stop=(a, z) == TERMS[-1], skip_group_check=True)
                    ins.then_inc(s_y, 1)

            rows(ROWS - 1, 1, [0, 1])
            layer0(0, 0)
            rows(ROWS - 1, 1, [2])
            pe.wait_ge(s_c3h, 1)
            pe.wait_ge(s_c3l, 1)
            pe.wait_ge(s_accl, ACC_A + OUT * (ROWS - 1) + OUT_AT[1])
            for s in range(2):
                block_products(0, s, False)
            with pe.Fori(1, NB // 2 - 1) as i:
                for s in range(2):
                    block_products(i, s, False)
            block_products(NB // 2 - 1, 0, False)
            block_products(NB // 2 - 1, 1, True)


_INS = ["x", "itok_B_0_15", "itok_B_0_2", "itok_B_0_7", "L0_cond_weights", "L1_cond_W", "L1_cond_lora_A", "L1_cond_lora_B",
        "L2_cond_W", "L2_cond_lora_A", "L2_cond_lora_B_w", "L3_cond_W", "L3_cond_Wr", "L3_cond_A", "L3_cond_B"]
_OUTS = [((32, 64, 1024), "float32")]


def kernel(**inputs):
    import numpy as _np
    import concourse.bacc as _bacc
    from concourse import mybir as _mybir
    from concourse.bass_utils import run_bass_kernel_spmd as _run

    nc = _bacc.Bacc("TRN2", target_bir_lowering=False, num_devices=1)
    arrays, args = {}, []
    for name in _INS:
        a = _np.ascontiguousarray(inputs[name])
        arrays[f"in_{name}_dram"] = a
        args.append(nc.dram_tensor(f"in_{name}_dram", a.shape, _mybir.dt.from_np(a.dtype), kind="ExternalInput").ap())
    for i, (shape, dtype) in enumerate(_OUTS):
        dt = _mybir.dt.from_np(_np.dtype(dtype))
        args.append(nc.dram_tensor(f"out_{i}_dram", shape, dt, kind="ExternalOutput").ap())
    cond_resid_kernel(nc, *args)
    r = _run(nc, [arrays], core_ids=[0])
    return r.results[0]["out_0_dram"]
```

```python
from contextlib import ExitStack

import concourse.bass as bass
from concourse import mybir

F32 = mybir.dt.float32
F32R = mybir.dt.float32r
I32 = mybir.dt.int32
U32 = mybir.dt.uint32
ALU = mybir.AluOpType
ACT = mybir.ActivationFunctionType

P = 128
BANK = 512
LANG_BIAS = 5.0
SCALE2 = 16 / 32
SCALE3 = 32.0 / 16.0


def cond_resid_kernel(nc, x, idx_adapter, idx_labeler, idx_language, w0, w1, a1, b1, w2, a2, b2, w3, wr, a3, b3, out):
    B, T, D = out.shape
    _, NA, _, R1 = a1.shape
    _, NL, _, R2 = a2.shape
    E = wr.shape[2]
    R3 = a3.shape[2] // E
    K = D // P
    PER = P // T
    NB = B // PER
    assert PER == 2 and K == 8 and D == 2 * BANK and E * R3 == P and NB % 2 == 0
    ER = E * R3
    C3 = ER + E
    A2C = NL * R2
    EC = C3 + A2C
    XC = D + EC
    SC = C3 + PER * (R2 + R1)
    SEG1 = 3 * R1
    SEG2 = 3 * R2
    LORA = NA * R1 // P
    ROWS = LORA + K
    F3C = 3 * P
    FCOLS = [(0, F3C), (F3C, 2 * F3C), (2 * F3C, D)]
    WIDTH_A = [F3C, F3C, D - 2 * F3C + C3]
    LABELERS = [range(3, NL), range(0), range(0, 3)]
    WIDTH = [w + R2 * len(n) for w, n in zip(WIDTH_A, LABELERS)]
    ORDER = [2, 0, 1]
    ACC_A = 3 * (K + 1)
    ACC_B = 3 * ROWS

    def f32(ap):
        return ap.bitcast(F32)

    def above(engine, semaphore, value):
        if not isinstance(value, int) or value > 0:
            engine.wait_ge(semaphore, value)

    def held(engine, value):
        if isinstance(value, int):
            return value
        register = engine.alloc_register()
        engine.reg_mov(register, value)
        return engine.snap(register)

    BASE = 16512
    X0, Y0, Z0 = BASE, BASE + 65536, BASE + 150016
    R0 = Z0 + 35328
    V0 = R0 + 3 * 4096
    Q0 = V0 + 8192

    def at(name, shape, dtype, offset):
        return nc.alloc_sbuf_tensor_at(name, shape, dtype, offset=offset)

    def pair(name, shape, offset):
        size = 4
        for n in shape[1:]:
            size *= n
        return at(name + "_hi", shape, F32R, offset), at(name + "_lo", shape, F32R, offset + size)

    EY = [Y0, Y0 + 8 * K * WIDTH[0], Y0 + 8 * K * (WIDTH[0] + WIDTH[1])]
    W2S = pair("w2s", [P, K, D], X0)
    M = pair("m", [P, K, D], X0)
    b1stage = [pair(f"b1stage{n}", [P, BANK], X0 + 4 * D * (K - 3 + n + (K - 3) * (n // 3))) for n in range(3 * LORA)]
    EX = [pair(f"e{c}", [P, K, WIDTH[c]], EY[c]) for c in range(3)]
    G = [pair(f"g{c}", [P, K, WIDTH_A[c]], at_) for c, at_ in enumerate((EY[1], Z0, EY[0]))]
    w2raw = [at(f"w2raw{k}", [P, D], F32, Z0 + 4096 * k) for k in range(K)]
    graw = [at(f"graw{c}", [P, K, WIDTH_A[c]], F32, at_) for c, at_ in enumerate((R0, R0, EY[2]))]
    b2raw = at("b2raw", [P, K, R2], F32, EY[2] + 4 * K * WIDTH_A[2])
    a2raw = at("a2raw", [P, NL, K, R2], F32, Z0 + 8 * K * WIDTH_A[1])
    TB = pair("tb", [P, K, EC], Z0)
    W1T = [pair("w1t0", [P, K, P], Z0 + 27136), pair("w1t1", [P, K, P], Z0 + 18944)]
    ost = [at(f"ost{s}", [P, D], F32, Z0 + 18944 + 4096 * s) for s in range(2)]
    raw = [at(f"raw{n}", [P, K, P], F32, R0 + 4096 * n) for n in range(2)]
    bdraw = [at(f"bdraw{s}", [P, P], F32, R0 + 8192 + 512 * s) for s in range(2)]
    BD = [pair(f"bd{s}", [P, P], R0 + 9216 + 1024 * s) for s in range(2)]
    a1raw = at("a1raw", [P, NA, K, R1], F32, V0)
    B2X = pair("b2x", [P, K, 3 * R2], V0)
    q = [Q0]

    def small(name, shape, dtype=F32):
        size = 4
        for n in shape[1:]:
            size *= n
        t = at(name, shape, dtype, q[0])
        q[0] += -(-size // 32) * 32
        return t

    ident = small("ident", [P, P])
    b2stage = small("b2stage", [SEG2, BANK], F32R)
    idx_a = small("idx_a", [1, B], I32)
    idx_l = small("idx_l", [1, B], I32)
    lang = small("lang", [P, B], I32)
    langf = small("langf", [P, NB])
    iota = small("iota", [P, E])
    bias = small("bias", [P, NB, E])
    lg = small("lg", [P, E])
    top = small("top", [P, 8])
    topi = small("topi", [P, 8], U32)
    topf = small("topf", [P, 2])
    ex = small("ex", [P, 1])
    den = small("den", [P, 1])
    gw = small("gw", [P, 2])
    gm = small("gm", [P, 2, E])
    gate = small("gate", [P, E])
    assert q[0] <= 229344

    q[0] = EY[2]
    XT = [(small(f"xt{s}_hi", [P, K, P], F32R), small(f"xt{s}_lo", [P, K, P], F32R)) for s in range(2)]
    S = (small("s_hi", [P, K, SC], F32R), small("s_lo", [P, K, SC], F32R))
    assert q[0] <= Z0
    q[0] = EY[0]
    b1s = [small(f"b1s{s}", [2 * SEG1, D + C3 + PER * R2], F32R) for s in range(2)]
    b2s = small("b2s", [SEG2, D + C3], F32R)
    XM = (small("xm_hi", [P, D], F32R), small("xm_lo", [P, D], F32R))
    XN = (small("xn_hi", [P, SC], F32R), small("xn_lo", [P, SC], F32R))
    h1c = small("h1c", [P, 2 * SEG1], F32R)
    h1T = small("h1T", [2 * SEG1, P], F32R)
    h2c = small("h2c", [P, 3, R2], F32R)
    h2T = small("h2T", [SEG2, P], F32R)
    gh = small("gh", [P, E, R3])
    GHT = (small("ght_hi", [P, P], F32R), small("ght_lo", [P, P], F32R))
    assert q[0] <= EY[1]
    q[0] = EY[1]
    b3raw = small("b3raw", [P, D])
    B3 = (small("b3_hi", [P, D], F32R), small("b3_lo", [P, D], F32R))
    assert q[0] <= EY[2]

    with ExitStack() as ctx:
        bank = [ctx.enter_context(nc.psum_tensor(f"bank{n}", [P, BANK], F32)) for n in range(8)]

        def sem(name):
            return ctx.enter_context(nc.semaphore(name))

        b1scr = nc.dram_tensor("b1scr", (NA, 2, R1, XC), F32).ap()
        b2scr = nc.dram_tensor("b2scr", (SEG2, D + C3), F32).ap()

        s_idx = sem("s_idx")
        s_b2r = sem("s_b2r")
        s_wr = sem("s_wr")
        s_in = [sem(f"s_in{k}") for k in range(K)]
        s_g3 = [sem(f"s_g3{n}") for n in range(4)]
        s_a2 = sem("s_a2")
        s_a1 = sem("s_a1")
        s_raw = [sem(f"s_raw{n}") for n in range(2)]
        s_id = sem("s_id")
        s_cst = sem("s_cst")
        s_diag = sem("s_diag")
        s_diag1 = sem("s_diag1")
        s_b2h = sem("s_b2h")
        s_b2l = sem("s_b2l")
        s_w2h = sem("s_w2h")
        s_w2l = sem("s_w2l")
        s_g3h = sem("s_g3h")
        s_g3l = sem("s_g3l")
        s_a2h = sem("s_a2h")
        s_a2l = sem("s_a2l")
        s_w1h = sem("s_w1h")
        s_w1l = sem("s_w1l")
        s_acc = sem("s_acc")
        s_acch = sem("s_acch")
        s_accl = sem("s_accl")
        s_b2st = sem("s_b2st")
        s_b1st = sem("s_b1st")
        s_bdz = sem("s_bdz")
        s_w0 = [sem(f"s_w0{n}") for n in range(2)]
        s_b1z = sem("s_b1z")
        s_b1s = [sem(f"s_b1s{n}") for n in range(2)]
        s_b2s = sem("s_b2s")
        s_b3 = sem("s_b3")
        s_b3h = sem("s_b3h")
        s_b3l = sem("s_b3l")
        s_bd = sem("s_bd")
        s_bdc = sem("s_bdc")
        s_s0h = sem("s_s0h")
        s_s0l = sem("s_s0l")
        s_sel = sem("s_sel")
        s_a1c = sem("s_a1c")
        s_z = sem("s_z")
        s_xth = sem("s_xth")
        s_xtl = sem("s_xtl")
        s_nar = sem("s_nar")
        s_xnh = sem("s_xnh")
        s_xnl = sem("s_xnl")
        s_wide = sem("s_wide")
        s_xmh = sem("s_xmh")
        s_xml = sem("s_xml")
        s_small = sem("s_small")
        s_h1c = sem("s_h1c")
        s_h2c = sem("s_h2c")
        s_ht = sem("s_ht")
        s_hts = sem("s_hts")
        s_ghl = sem("s_ghl")
        s_dc = sem("s_dc")
        s_top = sem("s_top")
        s_ex = sem("s_ex")
        s_gh = sem("s_gh")
        s_y = sem("s_y")
        s_yfree = [sem("s_yfree0"), sem("s_yfree1")]
        s_st = [sem(f"s_st{n}") for n in range(2)]

        PARTS = {2: ((0, D - 2 * F3C, M, 2 * F3C), (D - 2 * F3C, WIDTH[2], TB, 0)),
                 0: ((0, F3C, M, 0), (F3C, WIDTH[0], TB, WIDTH[2] - (D - 2 * F3C))), 1: ((0, F3C, M, F3C),)}
        OUT = sum(len(parts) for parts in PARTS.values())
        OUT_AT = [2, 4, 5]

        def in_place(b1scr_rows, c):
            runs = [(0, WIDTH[2])] if c == 2 else [(0, F3C)]
            places = [(lo, hi, b1scr_rows[:, :, :, COLUMN[c] + lo:COLUMN[c] + hi]) for lo, hi in runs]
            if c == 0:
                places.append((F3C, WIDTH[0], b1scr_rows[:, :, :, D + A2COL[0]:XC]))
            return places

        BETWEEN = {(0, 6): (8, 9, 10, 11), (0, 7): (12, 13, 14, 15), (1, 4): (16, 17, 18, 19), (1, 5): (20, 21, 22, 23)}
        OUTER = 6
        COLUMN = [0, F3C, 2 * F3C]
        A2COL = {2: C3, 0: C3 + 3 * R2}
        A2PART = [2, 0]

        def g_block(n):
            return ORDER[n // K], n % K

        IDENTITIES = [("g", n) if kind else ("w", n) for n in range(K) for kind in ((0, 1) if n >= 2 * F3C // P else (0,))] \
            + [("g", K + k) for k in range(3)] + [("g", 2 * K + 3 + k) for k in range(3)]
        DIAG = {it: n + 1 for n, it in enumerate(IDENTITIES)}

        def stage_bank(r, j):
            return bank[3 * (r % 2) + j]

        orows = out.rearrange("(n s) t d -> n (s t) d", s=PER)

        block = ctx.enter_context(nc.Block())

        @block.sync
        def _(sp):
            sp.dma_start(graw[2][:, :, WIDTH_A[2] - E:], wr).then_inc(s_wr, 16)
            for k in range(K):
                sp.dma_start(w2raw[k][:, :], w2[k * P:(k + 1) * P, :]).then_inc(s_in[k], 16)
                sp.dma_start(graw[2][:, k, 0:D - 2 * F3C], w3[k, :, 2 * F3C:]).then_inc(s_in[k], 16)
                sp.dma_start(graw[2][:, k, D - 2 * F3C:D - 2 * F3C + ER], a3[k]).then_inc(s_in[k], 16)
            sp.dma_start(b2raw[:, :, :], b2).then_inc(s_b2r, 16)

            def load_chunk(m):
                c = ORDER[m]
                for h in range(2):
                    if m == 2 and h == 0:
                        sp.wait_ge(s_g3l, 2 * K)
                    ks = slice(4 * h, 4 * h + 4)
                    sp.dma_start(graw[c][:, ks, :], w3[ks, :, COLUMN[c]:COLUMN[c] + F3C].rearrange("k p n -> p k n")
                                 ).then_inc(s_g3[2 * m - 2 + h], 16)

            load_chunk(1)
            sp.dma_start(idx_a[:, :], idx_adapter.rearrange("(a n) -> a n", a=1)).then_inc(s_idx, 16)
            sp.dma_start(idx_l[:, :], idx_labeler.rearrange("(a n) -> a n", a=1)).then_inc(s_idx, 16)
            sp.dma_start(lang[:, :], idx_language.partition_broadcast(P)).then_inc(s_idx, 16)
            sp.wait_ge(s_w2l, K)
            sp.dma_start(a2raw[:, :, :, :], a2).then_inc(s_a2, 16)
            load_chunk(2)

            def load_rows(r, u, src):
                if isinstance(r, int) and r < 2:
                    sp.wait_ge(s_g3l, 3 * K)
                else:
                    sp.wait_ge(s_w1l, r - 1)
                sp.dma_start(raw[u][:, :, :], src).then_inc(s_raw[u], 16)

            def w1_of(r):
                return w1[r - LORA] if isinstance(r, int) else w1[bass.ds(r - LORA, 1)].rearrange("a p k n -> p (a k) n")

            def store_lora(r):
                dst = b1scr[r * P // R1:(r + 1) * P // R1]
                for j, c in enumerate(ORDER):
                    sp.wait_ge(s_accl, ACC_A + OUT * r + OUT_AT[j])
                    for lo_, hi_, scr in in_place(dst, c):
                        for half in range(2):
                            sp.dma_start(scr[:, half], f32(b1stage[3 * r + j][half][:, lo_:hi_])).then_inc(s_b1st, 16)

            load_rows(0, 0, b1[0])
            load_rows(1, 1, b1[1])
            load_rows(2, 0, w1_of(2))
            sp.wait_ge(s_acc, ACC_A)
            sp.dma_start(a1raw[:, :, :, :], a1).then_inc(s_a1, 16)
            load_rows(3, 1, w1_of(3))
            store_lora(0)
            load_rows(4, 0, w1_of(4))
            load_rows(5, 1, w1_of(5))
            store_lora(1)
            with sp.Fori(3, ROWS // 2) as i:
                for u in range(2):
                    load_rows(2 * i + u, u, w1_of(2 * i + u))

            sp.wait_ge(s_idx, 48)

            def index(tile, n, count):
                return sp.value_load(tile[0:1, bass.ds(n, 1)], min_val=0, max_val=count - 1)

            def load_w0(b, s):
                for h in range(PER):
                    a = index(idx_a, PER * b + h, NA)
                    sp.dma_start(bdraw[s][h * T:(h + 1) * T, h * T:(h + 1) * T],
                                 w0[bass.ds(a, 1)].rearrange("a c d -> (a c) d")).then_inc(s_w0[s], 16)

            def load_b1s(b, s):
                for h in range(PER):
                    a = index(idx_a, PER * b + h, NA)
                    lab = index(idx_l, PER * b + h, NL)
                    both, again = slice(h * SEG1, h * SEG1 + 2 * R1), slice(h * SEG1 + 2 * R1, (h + 1) * SEG1)
                    for rows, halves in ((both, slice(0, 2)), (again, slice(0, 1))):
                        for cols, scr_cols in ((slice(0, D + C3), slice(0, D + C3)),
                                               (slice(D + C3 + h * R2, D + C3 + (h + 1) * R2), bass.ds(lab * R2 + (D + C3), R2))):
                            sp.dma_start(f32(b1s[s][rows, cols]),
                                         b1scr[bass.ds(a, 1), halves, :, scr_cols].rearrange("a s r c -> (a s r) c")
                                         ).then_inc(s_b1s[s], 16)

            sp.wait_ge(s_bdz, 2)
            load_w0(0, 0)
            load_w0(1, 1)
            for b in range(2):
                load_rows(ROWS + b, b, x[b])
            sp.wait_ge(s_b1st, 16 * 8 * LORA)
            sp.wait_ge(s_b2st, 16 * 3)
            sp.wait_ge(s_acc, ACC_A + ACC_B - 1)
            sp.wait_ge(s_b1z, 2)
            load_b1s(0, 0)
            sp.dma_start(f32(b2s[:, :]), b2scr).then_inc(s_b2s, 16)
            sp.wait_ge(s_acc, ACC_A + ACC_B)
            sp.dma_start(b3raw[:, :], b3).then_inc(s_b3, 16)
            load_b1s(1, 1)

            def block_io(i, s, last):
                b = 2 * i + s
                if not last:
                    sp.wait_ge(s_xtl, b + 1)
                    sp.dma_start(raw[s][:, :, :], x[bass.ds(b + 2, 1)].rearrange("a p k t -> p (a k) t")).then_inc(s_raw[s], 16)
                    sp.wait_ge(s_bd, b + 1)
                    load_w0(b + 2, s)
                sp.wait_ge(s_yfree[0], b + 1)
                sp.wait_ge(s_yfree[1], b + 1)
                if last:
                    sp.dma_start(orows[b], ost[s][:, :]).then_inc(s_st[s], 16)
                else:
                    sp.dma_start(orows[bass.ds(b, 1)].rearrange("a t d -> (a t) d"), ost[s][:, :]).then_inc(s_st[s], 16)
                if not last:
                    load_b1s(b + 2, s)

            for s in range(2):
                block_io(0, s, False)
            with sp.Fori(1, NB // 2 - 1) as i:
                for s in range(2):
                    block_io(i, s, False)
            for s in range(2):
                block_io(NB // 2 - 1, s, True)
            for s in range(2):
                sp.wait_ge(s_st[s], 16 * (NB // 2))

        @block.gpsimd
        def _(pool):
            nc.gpsimd.memset(ident[:, :], 0.0).then_inc(s_id, 1)
            pool.wait_ge(s_id, 1)
            nc.gpsimd.affine_select(out=ident[:, :], in_=ident[:, :], compare_op=ALU.not_equal, fill=1.0,
                                    base=0, pattern=[[-1, P]], channel_multiplier=1).then_inc(s_id, 1)
            pool.wait_ge(s_id, 2)

            def add_identities(items):
                for kind, n in items:
                    if kind == "w":
                        pool.wait_ge(s_in[n], 48)
                        blk = w2raw[n][:, n * P:(n + 1) * P]
                    else:
                        c, k = g_block(n)
                        if c == ORDER[0]:
                            pool.wait_ge(s_in[k], 48)
                        else:
                            pool.wait_ge(s_g3[2 * (n // K) - 2 + k // 4], 16)
                        blk = graw[c][:, k, (k % 3) * P:(k % 3 + 1) * P]
                    nc.gpsimd.tensor_tensor(blk, blk, ident[:, :], ALU.add).then_inc(s_diag, 1)

            def store_b2(m):
                c = ORDER[m]
                pool.wait_ge(s_accl, (K + 1) * (m + 1))
                pool.dma_start(b2scr[:, COLUMN[c]:COLUMN[c] + WIDTH_A[c]], f32(b2stage[:, 0:WIDTH_A[c]])).then_inc(s_b2st, 16)

            add_identities(IDENTITIES[:-3])
            store_b2(0)
            add_identities(IDENTITIES[-3:])
            store_b2(1)
            pool.wait_ge(s_g3l, 3 * K)
            for s in range(2):
                nc.gpsimd.memset(bdraw[s][:, :], 0.0).then_inc(s_bdz, 1)
            store_b2(2)

            def diagonal(i, s):
                b = 2 * i + s
                pool.wait_ge(s_w0[s], 32 * i + 32)
                nc.gpsimd.tensor_tensor(bdraw[s][:, :], bdraw[s][:, :], ident[:, :], ALU.add).then_inc(s_bdc, 1)
                there, free = held(pool, 2 * b + 1), held(pool, 2 * b - 2)
                pool.wait_ge(s_id, 2)
                above(pool, s_y, free)
                pool.wait_ge(s_bdc, there)
                nc.gpsimd.tensor_copy(BD[s][0][:, :], bdraw[s][:, :]).then_inc(s_bdc, 1)
                pool.wait_ge(s_bdc, 2 * b + 2)
                nc.gpsimd.tensor_tensor(BD[s][1][:, :], bdraw[s][:, :], f32(BD[s][0][:, :]), ALU.subtract).then_inc(s_bd, 1)

            def select(b):
                a = [pool.value_load(idx_a[0:1, bass.ds(PER * b + h, 1)], min_val=0, max_val=NA - 1) for h in range(PER)]
                l = [] if isinstance(b, int) and b == 0 else [pool.value_load(idx_l[0:1, bass.ds(PER * b + h, 1)], min_val=0, max_val=NL - 1) for h in range(PER)]
                a1_of = [a1raw[:, bass.ds(n, 1), :, :].rearrange("p a k r -> p (a k) r") for n in a]
                free, there = held(pool, b), held(pool, 2 * b + 2)
                pool.wait_ge(s_id, 2)
                above(pool, s_nar, free)
                for h in range(PER):
                    at_ = C3 + PER * R2 + h * R1
                    nc.gpsimd.tensor_copy(S[0][:, :, at_:at_ + R1], a1_of[h]).then_inc(s_a1c, 1)
                for h in range(len(l)):
                    at_ = C3 + h * R2
                    for z in range(2):
                        nc.gpsimd.tensor_copy(S[z][:, :, at_:at_ + R2],
                                              f32(TB[z])[:, :, bass.ds(l[h] * R2 + C3, R2)]).then_inc(s_sel, 1)
                pool.wait_ge(s_id, 2)
                pool.wait_ge(s_a1c, there)
                for h in range(PER):
                    at_ = C3 + PER * R2 + h * R1
                    nc.gpsimd.tensor_tensor(S[1][:, :, at_:at_ + R1], a1_of[h], f32(S[0][:, :, at_:at_ + R1]),
                                            ALU.subtract).then_inc(s_sel, 1)

            pool.wait_ge(s_idx, 48)
            pool.wait_ge(s_bdz, 2)
            pool.wait_ge(s_a1, 16)
            pool.wait_ge(s_acc, ACC_A + ACC_B - 2)
            select(0)
            diagonal(0, 0)
            pool.wait_ge(s_acc, ACC_A + ACC_B - 1)
            for s in range(2):
                nc.gpsimd.memset(f32(b1s[s][:, D + C3:]), 0.0).then_inc(s_b1z, 1)
            diagonal(0, 1)
            pool.wait_ge(s_accl, ACC_A + OUT * (ROWS - 1) + OUT_AT[1])
            select(1)
            diagonal(1, 0)
            select(2)
            diagonal(1, 1)
            with pool.Fori(1, NB // 2 - 1) as i:
                select(2 * i + 1)
                diagonal(i + 1, 0)
                select(2 * i + 2)
                diagonal(i + 1, 1)
            select(NB - 1)

        @block.scalar
        def _(act):
            def g_hi(n):
                c, k = g_block(n)
                if n < K:
                    act.wait_ge(s_in[k], 48)
                else:
                    act.wait_ge(s_g3[2 * (n // K) - 2 + k // 4], 16)
                if ("g", n) in DIAG:
                    act.wait_ge(s_diag, DIAG["g", n])
                nc.scalar.activation(G[c][0][:, k, :], graw[c][:, k, :], ACT.Copy).then_inc(s_g3h, 1)

            def w1_hi(r, u):
                if not (isinstance(r, int) and r == 0):
                    act.wait_ge(s_acc, ACC_A + 3 * (r - 1))
                if isinstance(r, int) and r < LORA:
                    act.wait_ge(s_raw[u], 16)
                else:
                    act.wait_ge(s_diag1, r - LORA + 1)
                nc.scalar.activation(W1T[u][0][:, :, :], raw[u][:, :, :], ACT.Copy).then_inc(s_w1h, 1)

            act.wait_ge(s_wr, 16)
            for k in range(K):
                g_hi(k)
                act.wait_ge(s_diag, DIAG["w", k])
                nc.scalar.activation(W2S[0][:, k, :], w2raw[k][:, :], ACT.Copy).then_inc(s_w2h, 1)
            act.wait_ge(s_b2r, 16)
            nc.scalar.activation(B2X[0][:, :, :].rearrange("p k (m r) -> p k m r", m=3),
                                 b2raw[:, :, :].unsqueeze(2).to_broadcast([P, K, 3, R2]), ACT.Copy).then_inc(s_b2h, 1)
            n = 0
            for m, c in enumerate(ORDER):
                w = WIDTH_A[c]
                for ob in range(K + 1):
                    for g in BETWEEN.get((m, ob), ()):
                        g_hi(g)
                    if m == 2 and ob in (1, 2):
                        part = A2PART[ob - 1]
                        ls, at_ = LABELERS[part], WIDTH_A[part]
                        act.wait_ge(s_a2, 16)
                        nc.scalar.activation(EX[part][0][:, :, at_:].rearrange("p k (l r) -> p l k r", r=R2),
                                             a2raw[:, ls[0]:ls[-1] + 1], ACT.Copy).then_inc(s_a2h, 1)
                    if m == 2 and ob == K:
                        act.wait_ge(s_a2l, 2)
                        w1_hi(0, 0)
                    if ob == K and m > 0:
                        act.wait_ge(s_b2st, 16 * m)
                    act.wait_ge(s_acc, n + 1)
                    if ob < K:
                        nc.scalar.activation(EX[c][0][:, ob, 0:w], bank[n % 6][:, 0:w], ACT.Copy).then_inc(s_acch, 1)
                    else:
                        nc.scalar.activation(b2stage[:, 0:w], bank[n % 6][0:SEG2, 0:w], ACT.Copy).then_inc(s_acch, 1)
                    n += 1

            def rows_hi(r, u, chunks=range(3)):
                for j in chunks:
                    act.wait_ge(s_id, 2)
                    act.wait_ge(s_acc, 3 * r + (ACC_A + j + 1))
                    for lo_, hi_, dst, at_ in PARTS[ORDER[j]]:
                        src = stage_bank(u, j)[:, lo_:hi_]
                        if isinstance(r, int) and r < LORA:
                            out_ = b1stage[3 * r + j][0][:, lo_:hi_]
                        else:
                            out_ = dst[0][:, bass.ds(r - LORA, 1), at_:at_ + hi_ - lo_].rearrange("p a n -> p (a n)")
                        nc.scalar.activation(out_, src, ACT.Copy).then_inc(s_acch, 1)

            w1_hi(1, 1)
            rows_hi(0, 0)
            w1_hi(2, 0)
            rows_hi(1, 1)
            with act.Fori(1, ROWS // 2 - 1) as i:
                w1_hi(2 * i + 1, 1)
                rows_hi(2 * i, 0)
                w1_hi(2 * i + 2, 0)
                act.wait_ge(s_b1st, 16 * 8 * LORA)
                rows_hi(2 * i + 1, 1)
            w1_hi(ROWS - 1, 1)
            rows_hi(ROWS - 2, 0)

            def xt_hi(i, s):
                b = 2 * i + s
                act.wait_ge(s_raw[s], 16 * i + 16 * (ROWS // 2 + 1))
                above(act, s_wide, 2 * b - 2)
                nc.scalar.activation(XT[s][0][:, :, :], raw[s][:, :, :], ACT.Copy).then_inc(s_xth, 1)

            def xn_hi(b):
                act.wait_ge(s_nar, b + 1)
                above(act, s_small, 3 * b - 2)
                nc.scalar.activation(XN[0][:, :], bank[4][:, 0:SC], ACT.Copy).then_inc(s_xnh, 1)

            def xm_hi(b, h):
                act.wait_ge(s_wide, 2 * b + h + 1)
                above(act, s_y, 2 * b)
                nc.scalar.activation(XM[0][:, h * BANK:(h + 1) * BANK], bank[h][:, :], ACT.Copy).then_inc(s_xmh, 1)

            def block_hi(i, s, last):
                b = 2 * i + s
                t = bank[5]
                if not last:
                    xt_hi(i + s, 1 - s)
                act.wait_ge(s_ht, 3 * b + 1)
                nc.scalar.activation(h1T[:, :], t[0:2 * SEG1, 0:P], ACT.Copy).then_inc(s_hts, 1)
                if isinstance(b, int) and b == 0:
                    act.wait_ge(s_b3, 16)
                    nc.scalar.activation(B3[0][:, :], b3raw[:, :], ACT.Copy).then_inc(s_b3h, 1)
                act.wait_ge(s_ht, 3 * b + 2)
                nc.scalar.activation(h2T[:, :], t[0:SEG2, P:2 * P], ACT.Copy).then_inc(s_hts, 1)
                xm_hi(b, 0)
                act.wait_ge(s_top, b + 1)
                nc.scalar.activation(ex[:, :], top[:, 0:1], ACT.Exp, bias=top[:, 1:2], scale=-1.0).then_inc(s_ex, 1)
                xm_hi(b, 1)
                act.wait_ge(s_ht, 3 * b + 3)
                nc.scalar.activation(GHT[0][:, :], t[:, 2 * P:3 * P], ACT.Copy).then_inc(s_hts, 1)
                if not last:
                    xn_hi(b + 1)
                act.wait_ge(s_y, 2 * b + 1)
                above(act, s_st[s], 16 * i)
                nc.scalar.activation(ost[s][:, 0:BANK], bank[2][:, :], ACT.Copy).then_inc(s_yfree[0], 1)

            rows_hi(ROWS - 1, 1, [0])
            xt_hi(0, 0)
            act.wait_ge(s_acch, ACC_A + OUT * (ROWS - 1) + OUT_AT[0])
            nc.scalar.activation(S[0][:, :, 0:C3], f32(TB[0])[:, :, 0:C3], ACT.Copy).then_inc(s_s0h, 1)
            act.wait_ge(s_idx, 48)
            labelers = [act.value_load(idx_l[0:1, h:h + 1], min_val=0, max_val=NL - 1) for h in range(PER)]
            rows_hi(ROWS - 1, 1, [1])
            for h in range(PER):
                act.wait_ge(s_acch, ACC_A + OUT * (ROWS - 1) + OUT_AT[1])
                nc.scalar.activation(S[0][:, :, C3 + h * R2:C3 + (h + 1) * R2],
                                     f32(TB[0])[:, :, bass.ds(labelers[h] * R2 + C3, R2)], ACT.Copy).then_inc(s_s0h, 1)
            rows_hi(ROWS - 1, 1, [2])
            xn_hi(0)
            for s in range(2):
                block_hi(0, s, False)
            with act.Fori(1, NB // 2 - 1) as i:
                for s in range(2):
                    block_hi(i, s, False)
            block_hi(NB // 2 - 1, 0, False)
            block_hi(NB // 2 - 1, 1, True)

        @block.vector
        def _(dve):
            V = nc.vector

            def lo(dst, src, hi, signal):
                V.tensor_tensor(dst, src, f32(hi), ALU.subtract).then_inc(signal, 1)

            def g_lo(n):
                c, k = g_block(n)
                dve.wait_ge(s_g3h, n + 1)
                lo(G[c][1][:, k, :], graw[c][:, k, :], G[c][0][:, k, :], s_g3l)

            def w1_lo(r, u):
                dve.wait_ge(s_w1h, r + 1)
                lo(W1T[u][1][:, :, :], raw[u][:, :, :], W1T[u][0][:, :, :], s_w1l)

            for k in range(K):
                g_lo(k)
                dve.wait_ge(s_w2h, k + 1)
                lo(W2S[1][:, k, :], w2raw[k][:, :], W2S[0][:, k, :], s_w2l)
            dve.wait_ge(s_b2h, 1)
            V.tensor_tensor(B2X[1][:, :, :].rearrange("p k (m r) -> p k m r", m=3),
                            b2raw[:, :, :].unsqueeze(2).to_broadcast([P, K, 3, R2]),
                            f32(B2X[0][:, :, :]).rearrange("p k (m r) -> p k m r", m=3), ALU.subtract).then_inc(s_b2l, 1)
            n = 0
            for m, c in enumerate(ORDER):
                w = WIDTH_A[c]
                for ob in range(K + 1):
                    for g in BETWEEN.get((m, ob), ()):
                        g_lo(g)
                    if m == 2 and ob in (1, 2):
                        part = A2PART[ob - 1]
                        ls, at_ = LABELERS[part], WIDTH_A[part]
                        dve.wait_ge(s_a2h, ob)
                        lo(EX[part][1][:, :, at_:].rearrange("p k (l r) -> p l k r", r=R2), a2raw[:, ls[0]:ls[-1] + 1],
                           EX[part][0][:, :, at_:].rearrange("p k (l r) -> p l k r", r=R2), s_a2l)
                    if m == 2 and ob == K:
                        w1_lo(0, 0)
                    dve.wait_ge(s_acch, n + 1)
                    if ob < K:
                        lo(EX[c][1][:, ob, 0:w], bank[n % 6][:, 0:w], EX[c][0][:, ob, 0:w], s_accl)
                    else:
                        mid = slice(R2, 2 * R2)
                        lo(b2stage[mid, 0:w], bank[n % 6][mid, 0:w], b2stage[mid, 0:w], s_accl)
                    n += 1

            def identity_rows(r, u):
                dve.wait_ge(s_raw[u], 8 * r + (16 - 8 * u))
                blk = raw[u][:, bass.ds(r - LORA, 1), :].rearrange("p a n -> p (a n)")
                V.tensor_tensor(blk, blk, ident[:, :], ALU.add).then_inc(s_diag1, 1)

            def rows_lo(r, u, chunks=range(3)):
                for j in chunks:
                    dve.wait_ge(s_acch, OUT * r + (ACC_A + OUT_AT[j]))
                    for lo_, hi_, dst, at_ in PARTS[ORDER[j]]:
                        if isinstance(r, int) and r < LORA:
                            hi, out_ = [b1stage[3 * r + j][z][:, lo_:hi_] for z in range(2)]
                        else:
                            hi, out_ = [dst[z][:, bass.ds(r - LORA, 1), at_:at_ + hi_ - lo_].rearrange("p a n -> p (a n)")
                                        for z in range(2)]
                        lo(out_, stage_bank(u, j)[:, lo_:hi_], hi, s_accl)

            dve.wait_ge(s_id, 2)
            w1_lo(1, 1)
            identity_rows(2, 0)
            rows_lo(0, 0)
            w1_lo(2, 0)
            identity_rows(3, 1)
            rows_lo(1, 1)
            for e in range(E):
                V.memset(iota[:, e:e + 1], float(e)).then_inc(s_cst, 1)
            dve.wait_ge(s_idx, 48)
            for h in range(PER):
                ts = slice(h * T, (h + 1) * T)
                V.tensor_copy(langf[ts, :], lang[ts, :].rearrange("p (t h) -> p h t", h=PER)[:, h, :]).then_inc(s_cst, 1)
            dve.wait_ge(s_cst, E + 2)
            V.tensor_tensor(bias[:, :, :], langf[:, :].unsqueeze(2).to_broadcast([P, NB, E]),
                            iota[:, :].unsqueeze(1).to_broadcast([P, NB, E]), ALU.is_equal).then_inc(s_cst, 1)
            dve.wait_ge(s_cst, E + 3)
            V.tensor_scalar(bias[:, :, :], bias[:, :, :], LANG_BIAS, None, ALU.mult).then_inc(s_cst, 1)
            with dve.Fori(1, ROWS // 2 - 1) as i:
                w1_lo(2 * i + 1, 1)
                identity_rows(2 * i + 2, 0)
                rows_lo(2 * i, 0)
                w1_lo(2 * i + 2, 0)
                identity_rows(2 * i + 3, 1)
                rows_lo(2 * i + 1, 1)
            w1_lo(ROWS - 1, 1)
            rows_lo(ROWS - 2, 0)

            def xt_lo(b, s):
                dve.wait_ge(s_xth, b + 1)
                lo(XT[s][1][:, :, :], raw[s][:, :, :], XT[s][0][:, :, :], s_xtl)

            def xn_lo(b):
                dve.wait_ge(s_xnh, b + 1)
                lo(XN[1][:, :], bank[4][:, 0:SC], XN[0][:, :], s_xnl)

            def xm_lo(b, h):
                dve.wait_ge(s_xmh, 2 * b + h + 1)
                cols = slice(h * BANK, (h + 1) * BANK)
                lo(XM[1][:, cols], bank[h][:, :], XM[0][:, cols], s_xml)

            STEPS = 13

            def block_lo(i, s, last):
                b = 2 * i + s
                nar = bank[6]
                done = [0]

                def then(ins):
                    ins.then_inc(s_dc, 1)
                    done[0] += 1

                def hold():
                    dve.wait_ge(s_dc, STEPS * b + done[0])

                dve.wait_ge(s_small, 3 * b + 1)
                for h in range(PER):
                    ts, at_ = slice(h * T, (h + 1) * T), C3 + PER * R2 + h * R1
                    then(V.tensor_copy(h1c[ts, h * SEG1:h * SEG1 + 2 * R1].rearrange("p (m r) -> p m r", m=2),
                                       nar[ts, at_:at_ + R1].unsqueeze(1).to_broadcast([T, 2, R1])))
                hold()
                for h in range(PER):
                    ts, at_ = slice(h * T, (h + 1) * T), C3 + PER * R2 + h * R1
                    lo(h1c[ts, h * SEG1 + 2 * R1:(h + 1) * SEG1], nar[ts, at_:at_ + R1], h1c[ts, h * SEG1:h * SEG1 + R1], s_h1c)
                if not last:
                    xt_lo(b + 1, 1 - s)
                if isinstance(b, int) and b == 0:
                    dve.wait_ge(s_b3h, 1)
                    lo(B3[1][:, :], b3raw[:, :], B3[0][:, :], s_b3l)
                dve.wait_ge(s_small, 3 * b + 2)
                for h in range(PER):
                    ts, at_ = slice(h * T, (h + 1) * T), C3 + h * R2
                    then(V.tensor_scalar(h2c[ts, 0:2, :], nar[ts, at_:at_ + R2].unsqueeze(1).to_broadcast([T, 2, R2]),
                                         SCALE2, None, ALU.mult))
                hold()
                for h in range(PER):
                    ts, at_ = slice(h * T, (h + 1) * T), C3 + h * R2
                    V.scalar_tensor_tensor(h2c[ts, 2, :], nar[ts, at_:at_ + R2], SCALE2, f32(h2c[ts, 0, :]),
                                           ALU.mult, ALU.subtract).then_inc(s_h2c, 1)
                xm_lo(b, 0)
                dve.wait_ge(s_small, 3 * b + 3)
                then(V.tensor_tensor(lg[:, :], nar[:, ER:C3], bias[:, bass.ds(b, 1), :].rearrange("p a e -> p (a e)"), ALU.add))
                logits_there, top_there = held(dve, STEPS * b + done[0]), held(dve, b + 1)
                dve.wait_ge(s_id, 2)
                dve.wait_ge(s_dc, logits_there)
                V.max(top[:, :], lg[:, :]).then_inc(s_top, 1)
                dve.wait_ge(s_id, 2)
                dve.wait_ge(s_top, top_there)
                then(V.max_index(topi[:, :], top[:, :], lg[:, :]))
                hold()
                then(V.tensor_copy(topf[:, :], topi[:, 0:2]))
                dve.wait_ge(s_ex, b + 1)
                then(V.tensor_scalar(den[:, :], ex[:, :], 1.0, 1.0 / SCALE3, ALU.add, ALU.mult))
                hold()
                then(V.reciprocal(gw[:, 0:1], den[:, :]))
                hold()
                then(V.tensor_tensor(gw[:, 1:2], gw[:, 0:1], ex[:, :], ALU.mult))
                hold()
                for m in range(2):
                    then(V.tensor_scalar(gm[:, m, :], iota[:, :], topf[:, m:m + 1], gw[:, m:m + 1], ALU.is_equal, ALU.mult))
                hold()
                then(V.tensor_tensor(gate[:, :], gm[:, 0, :], gm[:, 1, :], ALU.add))
                hold()
                V.tensor_tensor(gh[:, :, :], nar[:, 0:ER].rearrange("p (e r) -> p e r", e=E),
                                gate[:, :].unsqueeze(2).to_broadcast([P, E, R3]), ALU.mult).then_inc(s_gh, 1)
                assert done[0] == STEPS, done
                xm_lo(b, 1)
                dve.wait_ge(s_hts, 3 * b + 3)
                lo(GHT[1][:, :], bank[5][:, 2 * P:3 * P], GHT[0][:, :], s_ghl)
                if not last:
                    xn_lo(b + 1)
                dve.wait_ge(s_y, 2 * b + 2)
                above(dve, s_st[s], 16 * i)
                V.tensor_copy(ost[s][:, BANK:], bank[3][:, :]).then_inc(s_yfree[1], 1)

            rows_lo(ROWS - 1, 1, [0])
            xt_lo(0, 0)
            dve.wait_ge(s_accl, ACC_A + OUT * (ROWS - 1) + OUT_AT[0])
            V.tensor_copy(S[1][:, :, 0:C3], f32(TB[1])[:, :, 0:C3]).then_inc(s_s0l, 1)
            labelers = [dve.value_load(idx_l[0:1, h:h + 1], min_val=0, max_val=NL - 1) for h in range(PER)]
            rows_lo(ROWS - 1, 1, [1])
            for h in range(PER):
                dve.wait_ge(s_accl, ACC_A + OUT * (ROWS - 1) + OUT_AT[1])
                V.tensor_copy(S[1][:, :, C3 + h * R2:C3 + (h + 1) * R2],
                              f32(TB[1])[:, :, bass.ds(labelers[h] * R2 + C3, R2)]).then_inc(s_s0l, 1)
            V.memset(f32(h1c[:, :]), 0.0).then_inc(s_z, 1)
            rows_lo(ROWS - 1, 1, [2])
            xn_lo(0)
            dve.wait_ge(s_z, 1)
            dve.wait_ge(s_cst, E + 4)
            for s in range(2):
                block_lo(0, s, False)
            with dve.Fori(1, NB // 2 - 1) as i:
                for s in range(2):
                    block_lo(i, s, False)
            block_lo(NB // 2 - 1, 0, False)
            block_lo(NB // 2 - 1, 1, True)

        @block.tensor
        def _(pe):
            TERMS = ((0, 0), (0, 1), (1, 0))

            def product(to, ob, c, ks):
                w, rows = WIDTH_A[c], slice(0, P if ob < K else SEG2)
                for k in ks:
                    for a, z in TERMS:
                        lhs = W2S[a][:, k, ob * P:(ob + 1) * P] if ob < K else B2X[a][:, k, :]
                        ins = nc.tensor.matmul(to[rows, 0:w], lhs, G[c][z][:, k, 0:w], start=(k == 0 and (a, z) == TERMS[0]),
                                               stop=(k == K - 1 and (a, z) == TERMS[-1]), skip_group_check=True)
                return ins

            for k in range(K):
                pe.wait_ge(s_g3l, k + 1)
                pe.wait_ge(s_w2l, k + 1)
                for ob in range(OUTER):
                    ins = product(bank[ob], ob, ORDER[0], [k])
                    if k == K - 1:
                        ins.then_inc(s_acc, 1)
            n = OUTER
            for m, c in enumerate(ORDER):
                for ob in range(OUTER if m == 0 else 0, K + 1):
                    if m > 0 and ob == 0:
                        pe.wait_ge(s_g3l, K * (m + 1))
                    if m == 0 and ob == K:
                        pe.wait_ge(s_b2l, 1)
                    pe.wait_ge(s_accl, n - 5)
                    product(bank[n % 6], ob, c, range(K)).then_inc(s_acc, 1)
                    n += 1

            def rows(r, u, chunks=range(3)):
                for j in chunks:
                    c = ORDER[j]
                    if j == 0:
                        pe.wait_ge(s_w1l, r + 1)
                    if isinstance(r, int) and r == 0:
                        pe.wait_ge(s_accl, ACC_A - 2 + j)
                    elif not (isinstance(r, int) and r == 1):
                        pe.wait_ge(s_accl, OUT * r + (ACC_A - 2 * OUT + OUT_AT[j]))
                    for k in range(K):
                        for a, z in TERMS:
                            ins = nc.tensor.matmul(stage_bank(u, j)[:, 0:WIDTH[c]], W1T[u][a][:, k, :], EX[c][z][:, k, :],
                                                   start=(k == 0 and (a, z) == TERMS[0]), stop=(k == K - 1 and (a, z) == TERMS[-1]))
                    ins.then_inc(s_acc, 1)

            pe.wait_ge(s_a2l, 2)
            rows(0, 0)
            rows(1, 1)
            with pe.Fori(1, ROWS // 2) as i:
                rows(2 * i, 0)
                rows(2 * i + 1, 1)

            def narrow(b, s, part):
                if part == 0:
                    pe.wait_ge(s_xtl, b + 1)
                    pe.wait_ge(s_sel, 6 * b + 2)
                    above(pe, s_xnl, b)
                for k in (range(K // 2), range(K // 2, K))[part]:
                    for a, z in TERMS:
                        ins = nc.tensor.matmul(bank[4][:, 0:SC], XT[s][a][:, k, :], S[z][:, k, :], start=(k == 0 and (a, z) == TERMS[0]),
                                               stop=(k == K - 1 and (a, z) == TERMS[-1]), skip_group_check=True)
                if part == 1:
                    ins.then_inc(s_nar, 1)

            def block_products(i, s, last):
                b = 2 * i + s
                first = isinstance(b, int) and b == 0
                res, t = bank[6], bank[5]
                wide = [(c, k, a, z) for c in range(2) for k in range(K) for a, z in TERMS]

                def run(lo_, hi_):
                    for c, k, a, z in wide[lo_:hi_]:
                        ins = nc.tensor.matmul(bank[c][:, :], XT[s][a][:, k, :], M[z][:, k, c * BANK:(c + 1) * BANK],
                                               start=(k == 0 and (a, z) == TERMS[0]), stop=(k == K - 1 and (a, z) == TERMS[-1]),
                                               skip_group_check=True)
                        if (k, a, z) == (K - 1,) + TERMS[-1]:
                            ins.then_inc(s_wide, 1)

                run(0, 5)
                pe.wait_ge(s_bd, b + 1)
                pe.wait_ge(s_xnl, b + 1)
                above(pe, s_gh, b)
                for a, z in TERMS:
                    ins = nc.tensor.matmul(res[:, 0:SC], BD[s][a][:, :], XN[z][:, :], start=(a, z) == TERMS[0],
                                           stop=(a, z) == TERMS[-1], skip_group_check=True)
                ins.then_inc(s_small, 1)
                run(5, 10)
                pe.wait_ge(s_h1c, 2 * b + 2)
                above(pe, s_ghl, b)
                nc.tensor.transpose(t[0:2 * SEG1, 0:P], f32(h1c[:, :]), ident[:, :]).then_inc(s_ht, 1)
                run(10, 14)
                pe.wait_ge(s_hts, 3 * b + 1)
                pe.wait_ge(s_b1s[s], 128 * i + 128)
                nc.tensor.matmul(res[:, 0:C3 + PER * R2], h1T[:, :], b1s[s][:, D:], start=False, stop=True,
                                 skip_group_check=True).then_inc(s_small, 1)
                run(14, 22)
                pe.wait_ge(s_h2c, 2 * b + 2)
                nc.tensor.transpose(t[0:SEG2, P:2 * P], f32(h2c[:, :, :]).rearrange("p m r -> p (m r)"), ident[:, :]).then_inc(s_ht, 1)
                run(22, 26)
                pe.wait_ge(s_hts, 3 * b + 2)
                if first:
                    pe.wait_ge(s_b2s, 16)
                nc.tensor.matmul(res[:, 0:C3], h2T[:, :], b2s[:, D:D + C3], start=False, stop=True,
                                 skip_group_check=True).then_inc(s_small, 1)
                run(26, 48)
                if not last:
                    narrow(b + 1, 1 - s, 0)
                pe.wait_ge(s_gh, b + 1)
                nc.tensor.transpose(t[:, 2 * P:3 * P], gh[:, :, :].rearrange("p e r -> p (e r)"), ident[:, :]).then_inc(s_ht, 1)
                if not last:
                    narrow(b + 1, 1 - s, 1)
                halves = [slice(c * BANK, (c + 1) * BANK) for c in range(2)]
                for c in range(2):
                    above(pe, s_yfree[c], b)
                    nc.tensor.matmul(bank[2 + c][:, :], h1T[:, :], b1s[s][:, halves[c]], start=True, stop=False, skip_group_check=True)
                    nc.tensor.matmul(bank[2 + c][:, :], h2T[:, :], b2s[:, halves[c]], start=False, stop=False, skip_group_check=True)
                pe.wait_ge(s_xml, 2 * b + 2)
                for c in range(2):
                    for a, z in TERMS:
                        nc.tensor.matmul(bank[2 + c][:, :], BD[s][a][:, :], XM[z][:, halves[c]], start=False, stop=False,
                                         skip_group_check=True)
                pe.wait_ge(s_ghl, b + 1)
                if first:
                    pe.wait_ge(s_b3l, 1)
                for c in range(2):
                    for a, z in TERMS:
                        ins = nc.tensor.matmul(bank[2 + c][:, :], GHT[a][:, :], B3[z][:, halves[c]], start=False,
                                               stop=(a, z) == TERMS[-1], skip_group_check=True)
                    ins.then_inc(s_y, 1)

            pe.wait_ge(s_s0h, 1 + PER)
            pe.wait_ge(s_s0l, 1 + PER)
            pe.wait_ge(s_accl, ACC_A + OUT * (ROWS - 1) + OUT_AT[1])
            narrow(0, 0, 0)
            narrow(0, 0, 1)
            pe.wait_ge(s_accl, ACC_A + OUT * ROWS)
            for s in range(2):
                block_products(0, s, False)
            with pe.Fori(1, NB // 2 - 1) as i:
                for s in range(2):
                    block_products(i, s, False)
            block_products(NB // 2 - 1, 0, False)
            block_products(NB // 2 - 1, 1, True)


_INS = ["x", "itok_B_0_15", "itok_B_0_2", "itok_B_0_7", "L0_cond_weights", "L1_cond_W", "L1_cond_lora_A", "L1_cond_lora_B",
        "L2_cond_W", "L2_cond_lora_A", "L2_cond_lora_B_w", "L3_cond_W", "L3_cond_Wr", "L3_cond_A", "L3_cond_B"]
_OUTS = [((32, 64, 1024), "float32")]


def lay_out(name, a):
    import numpy as _np

    if name == "x":
        a = a.reshape(-1, P, a.shape[2] // P, P).transpose(0, 3, 2, 1)
    elif name == "L1_cond_W":
        a = a.reshape(-1, P, a.shape[1] // P, P).transpose(0, 3, 2, 1)
    elif name == "L1_cond_lora_B":
        a = a.reshape(-1, P, a.shape[2] // P, P).transpose(0, 3, 2, 1)
    elif name in ("L1_cond_lora_A", "L2_cond_lora_A"):
        a = a.reshape(a.shape[0], -1, P, a.shape[2]).transpose(2, 0, 1, 3)
    elif name == "L2_cond_lora_B_w":
        a = a.reshape(-1, P, a.shape[1]).transpose(1, 0, 2)
    elif name == "L3_cond_W":
        a = a.T.reshape(-1, P, a.shape[0])
    elif name == "L3_cond_Wr":
        a = a.T.reshape(-1, P, a.shape[0]).transpose(1, 0, 2)
    elif name == "L3_cond_A":
        a = a.transpose(2, 0, 1).reshape(-1, P, a.shape[0] * a.shape[1])
    elif name == "L3_cond_B":
        a = a.transpose(0, 2, 1).reshape(-1, a.shape[1])
    return _np.ascontiguousarray(a)


def kernel(**inputs):
    import numpy as _np
    import concourse.bacc as _bacc
    from concourse import mybir as _mybir
    from concourse.bass_utils import run_bass_kernel_spmd as _run

    nc = _bacc.Bacc("TRN2", target_bir_lowering=False, num_devices=1)
    arrays, args = {}, []
    for name in _INS:
        a = lay_out(name, _np.asarray(inputs[name]))
        arrays[f"in_{name}_dram"] = a
        args.append(nc.dram_tensor(f"in_{name}_dram", a.shape, _mybir.dt.from_np(a.dtype), kind="ExternalInput").ap())
    for i, (shape, dtype) in enumerate(_OUTS):
        dt = _mybir.dt.from_np(_np.dtype(dtype))
        args.append(nc.dram_tensor(f"out_{i}_dram", shape, dt, kind="ExternalOutput").ap())
    cond_resid_kernel(nc, *args)
    r = _run(nc, [arrays], core_ids=[0])
    return r.results[0]["out_0_dram"]
```
